# Optimizing a Trainium2 kernel written in Bass

```python
import numpy as np
import jax
import jax.numpy as jnp

def _softmax(x, axis=-1):
    return jax.nn.softmax(x, axis=axis)

def _gelu(x):
    return jax.nn.gelu(x, approximate=True)

def _silu(x):
    return jax.nn.silu(x)

def _sigmoid(x):
    return jax.nn.sigmoid(x)

def _layernorm(x, axis=-1, eps=1e-05):
    m = jnp.mean(x, axis=axis, keepdims=True)
    v = jnp.var(x, axis=axis, keepdims=True)
    return (x - m) / jnp.sqrt(v + eps)

def _scatter_add(tgt, idx, src, axis=0):
    return tgt.at[idx].add(src)

def _segment_sum(src, seg, n):
    return jax.ops.segment_sum(src, seg, n)
kernel_name = 'mk_seq_preln_d1_jaxref_r8_a9350a'

def setup_inputs(seed: int=0):
    np.random.seed(seed)
    _w = jnp.asarray

    def _L0_attn_setup():
        import math
        import jax, jax.numpy as jnp
        import numpy as np
        NHEAD = 16
        HEAD_DIM = 64
        D_MODEL = 128
        B, T = (2, 512)

        def _cosformer(x, Wq, bq, Wk, bk, Wv, bv, Wo, bo):
            Bsz, Tlen, _ = x.shape
            H, dh = (NHEAD, HEAD_DIM)
            Q = (x @ Wq + bq).reshape(Bsz, Tlen, H, dh)
            K = (x @ Wk + bk).reshape(Bsz, Tlen, H, dh)
            V = (x @ Wv + bv).reshape(Bsz, Tlen, H, dh)
            Qp = jax.nn.relu(Q)
            Kp = jax.nn.relu(K)
            angles = math.pi / (2.0 * Tlen) * jnp.arange(Tlen, dtype=jnp.float32)
            cosw = jnp.cos(angles)[None, :, None, None]
            sinw = jnp.sin(angles)[None, :, None, None]
            Qc, Qs = (Qp * cosw, Qp * sinw)
            Kc, Ks = (Kp * cosw, Kp * sinw)
            tm = lambda a: jnp.moveaxis(a, 1, 0)
            Qc, Qs, Kc, Ks, Vt = (tm(Qc), tm(Qs), tm(Kc), tm(Ks), tm(V))
            S0 = jnp.zeros((Bsz, H, dh, dh), dtype=x.dtype)
            z0 = jnp.zeros((Bsz, H, dh), dtype=x.dtype)

            def step(carry, inp):
                S_cos, S_sin, z_cos, z_sin = carry
                qc, qs, kc, ks_, v = inp
                S_cos = S_cos + kc[..., :, None] * v[..., None, :]
                S_sin = S_sin + ks_[..., :, None] * v[..., None, :]
                z_cos = z_cos + kc
                z_sin = z_sin + ks_
                num = jnp.einsum('bhi,bhij->bhj', qc, S_cos) + jnp.einsum('bhi,bhij->bhj', qs, S_sin)
                den = jnp.sum(qc * z_cos + qs * z_sin, axis=-1)
                den = jnp.maximum(den, 1e-06)[..., None]
                return ((S_cos, S_sin, z_cos, z_sin), num / den)
            _, out = jax.lax.scan(step, (S0, S0, z0, z0), (Qc, Qs, Kc, Ks, Vt))
            out = jnp.moveaxis(out, 0, 1).reshape(Bsz, Tlen, H * dh)
            return out @ Wo + bo
        key = jax.random.key(seed)
        ks = jax.random.split(key, 9)
        HD = NHEAD * HEAD_DIM
        s_in = 1.0 / math.sqrt(D_MODEL)
        s_out = 1.0 / math.sqrt(HD)
        return {'x': jax.random.normal(ks[0], (B, T, D_MODEL), dtype=jnp.float32), 'Wq': jax.random.normal(ks[1], (D_MODEL, HD), dtype=jnp.float32) * s_in, 'bq': jnp.zeros((HD,), dtype=jnp.float32), 'Wk': jax.random.normal(ks[2], (D_MODEL, HD), dtype=jnp.float32) * s_in, 'bk': jnp.zeros((HD,), dtype=jnp.float32), 'Wv': jax.random.normal(ks[3], (D_MODEL, HD), dtype=jnp.float32) * s_in, 'bv': jnp.zeros((HD,), dtype=jnp.float32), 'Wo': jax.random.normal(ks[4], (HD, D_MODEL), dtype=jnp.float32) * s_out, 'bo': jnp.zeros((D_MODEL,), dtype=jnp.float32)}
    _L0_attn_in = _L0_attn_setup()

    def _L0_ffn_setup():
        import jax, jax.numpy as jnp
        import numpy as np
        B, S, D, E, F, TOP_K = (4, 256, 128, 8, 512, 2)
        key = jax.random.key(seed)
        k0, k1, k2, k3 = jax.random.split(key, 4)
        init = lambda k, shape, fan: (jax.random.normal(k, shape, jnp.float32) / np.sqrt(fan)).astype(jnp.float32)
        return {'x': jax.random.normal(k0, (B, S, D), jnp.float32), 'gate_w': init(k1, (D, E), D), 'w1': init(k2, (E, D, F), D), 'b1': jnp.zeros((E, F), jnp.float32), 'w2': init(k3, (E, F, D), F), 'b2': jnp.zeros((E, D), jnp.float32)}
    _L0_ffn_in = _L0_ffn_setup()
    _d = {'L0_attn_x': _L0_attn_in['x'], 'L0_attn_Wq': _L0_attn_in['Wq'], 'L0_attn_bq': _L0_attn_in['bq'], 'L0_attn_Wk': _L0_attn_in['Wk'], 'L0_attn_bk': _L0_attn_in['bk'], 'L0_attn_Wv': _L0_attn_in['Wv'], 'L0_attn_bv': _L0_attn_in['bv'], 'L0_attn_Wo': _L0_attn_in['Wo'], 'L0_attn_bo': _L0_attn_in['bo'], 'L0_ffn_gate_w': _L0_ffn_in['gate_w'], 'L0_ffn_w1': _L0_ffn_in['w1'], 'L0_ffn_b1': _L0_ffn_in['b1'], 'L0_ffn_w2': _L0_ffn_in['w2'], 'L0_ffn_b2': _L0_ffn_in['b2']}
    _x0 = _d['L0_attn_x']
    _d['L0_attn_x'] = jax.random.normal(jax.random.fold_in(jax.random.key(seed), 1), (1, 2048, 128), dtype=_x0.dtype)
    del _x0
    return _d

def reference(L0_attn_x, L0_attn_Wq, L0_attn_bq, L0_attn_Wk, L0_attn_bk, L0_attn_Wv, L0_attn_bv, L0_attn_Wo, L0_attn_bo, L0_ffn_gate_w, L0_ffn_w1, L0_ffn_b1, L0_ffn_w2, L0_ffn_b2):

    def _L0_attn_ref(x, Wq, bq, Wk, bk, Wv, bv, Wo, bo):
        import math
        import jax, jax.numpy as jnp
        import numpy as np
        NHEAD = 16
        HEAD_DIM = 64
        D_MODEL = 128
        B, T = (2, 512)

        def _cosformer(x, Wq, bq, Wk, bk, Wv, bv, Wo, bo):
            Bsz, Tlen, _ = x.shape
            H, dh = (NHEAD, HEAD_DIM)
            Q = (x @ Wq + bq).reshape(Bsz, Tlen, H, dh)
            K = (x @ Wk + bk).reshape(Bsz, Tlen, H, dh)
            V = (x @ Wv + bv).reshape(Bsz, Tlen, H, dh)
            Qp = jax.nn.relu(Q)
            Kp = jax.nn.relu(K)
            angles = math.pi / (2.0 * Tlen) * jnp.arange(Tlen, dtype=jnp.float32)
            cosw = jnp.cos(angles)[None, :, None, None]
            sinw = jnp.sin(angles)[None, :, None, None]
            Qc, Qs = (Qp * cosw, Qp * sinw)
            Kc, Ks = (Kp * cosw, Kp * sinw)
            tm = lambda a: jnp.moveaxis(a, 1, 0)
            Qc, Qs, Kc, Ks, Vt = (tm(Qc), tm(Qs), tm(Kc), tm(Ks), tm(V))
            S0 = jnp.zeros((Bsz, H, dh, dh), dtype=x.dtype)
            z0 = jnp.zeros((Bsz, H, dh), dtype=x.dtype)

            def step(carry, inp):
                S_cos, S_sin, z_cos, z_sin = carry
                qc, qs, kc, ks_, v = inp
                S_cos = S_cos + kc[..., :, None] * v[..., None, :]
                S_sin = S_sin + ks_[..., :, None] * v[..., None, :]
                z_cos = z_cos + kc
                z_sin = z_sin + ks_
                num = jnp.einsum('bhi,bhij->bhj', qc, S_cos) + jnp.einsum('bhi,bhij->bhj', qs, S_sin)
                den = jnp.sum(qc * z_cos + qs * z_sin, axis=-1)
                den = jnp.maximum(den, 1e-06)[..., None]
                return ((S_cos, S_sin, z_cos, z_sin), num / den)
            _, out = jax.lax.scan(step, (S0, S0, z0, z0), (Qc, Qs, Kc, Ks, Vt))
            out = jnp.moveaxis(out, 0, 1).reshape(Bsz, Tlen, H * dh)
            return out @ Wo + bo
        return _cosformer(x, Wq, bq, Wk, bk, Wv, bv, Wo, bo)

    def _L0_ffn_ref(x, gate_w, w1, b1, w2, b2):
        import jax, jax.numpy as jnp
        import numpy as np
        B, S, D, E, F, TOP_K = (4, 256, 128, 8, 512, 2)
        b, s, d = x.shape
        e = gate_w.shape[1]
        xf = x.reshape(-1, d)
        t = xf.shape[0]
        logits = xf @ gate_w
        top_w, top_idx = jax.lax.top_k(logits, TOP_K)
        top_w = jax.nn.softmax(top_w.astype(jnp.float32), axis=-1).astype(x.dtype)
        combine = jnp.zeros((t, e), x.dtype).at[jnp.arange(t)[:, None], top_idx].add(top_w)
        h = jax.nn.gelu(jnp.einsum('td,edf->tef', xf, w1) + b1, approximate=False)
        y = jnp.einsum('tef,efd->ted', h, w2) + b2
        out = jnp.einsum('ted,te->td', y, combine)
        return out.reshape(b, s, d)
    x = L0_attn_x
    x = x + _L0_attn_ref(_layernorm(x, axis=-1), L0_attn_Wq, L0_attn_bq, L0_attn_Wk, L0_attn_bk, L0_attn_Wv, L0_attn_bv, L0_attn_Wo, L0_attn_bo)
    x = x + _L0_ffn_ref(_layernorm(x, axis=-1), L0_ffn_gate_w, L0_ffn_w1, L0_ffn_b1, L0_ffn_w2, L0_ffn_b2)
    return x

_drawn_inputs = setup_inputs


def setup_inputs(seed=0):
    import zlib

    import numpy as np

    out = dict(_drawn_inputs(seed))
    spreads = {'L0_attn_bq': (0.0, 0.836),
     'L0_attn_bk': (0.0, 1.089),
     'L0_attn_bv': (0.0, 0.1),
     'L0_attn_bo': (0.0, 0.1),
     'L0_ffn_b1': (0.0, 0.1),
     'L0_ffn_b2': (0.0, 0.1)}
    factors = {}
    for name, (base, spread) in spreads.items():
        noise = np.random.default_rng([zlib.crc32(name.encode()), seed]).standard_normal(out[name].shape)
        drawn = base * np.exp(spread * noise) if base else spread * noise
        out[name] = jnp.asarray(drawn.astype(out[name].dtype))
    for name, factor in factors.items():
        out[name] = (out[name] * factor).astype(out[name].dtype)
    return out
```

```python
import math
from contextlib import ExitStack

import numpy as np

import concourse.bass as bass
from concourse import mybir

ALU = mybir.AluOpType
ACT = mybir.ActivationFunctionType
F32 = mybir.dt.float32
F32R = mybir.dt.float32r
U32 = mybir.dt.uint32

P = 128
T, D = 2048, 128
H, DH = 16, 64
HD = H * DH
E, F = 8, 512
EPS = 1e-5
DEN_MIN = 1e-6
NC = T // P
SC = 4
NS = NC // SC
ST = SC * P
NP = H // 2
VW = DH + 1
CS = 2 * VW
GH = 4
NG = H // GH
FB = F // P
EJ = 2

QK_JOBS = 2 * NP
KN_JOBS = 2 * SC
BIG_JOBS = QK_JOBS + KN_JOBS
V_JOBS = 2 * SC
GROUPS = SC * NG
STEPS = EJ * NS


def moe_block(nc, x, Wq, bq, Wk, bk, Wv, bv, Wo, bo, gate_w, w1, b1, w2, b2,
              c_rot, c_mask, c_ident, c_iota, out):
    with ExitStack() as ctx:
        def sb(name, shape, dt=F32):
            return ctx.enter_context(nc.sbuf_tensor(name, shape, dt))

        def sem(name):
            return ctx.enter_context(nc.semaphore(name))

        ps = ctx.enter_context(nc.psum_tensor("ps", [P, 8, 512], F32))

        x_sb = sb("x_sb", [P, NC, D])
        w_hi = [sb(f"w_hi{k}", [P, HD], F32R) for k in range(3)]
        w_lo = [sb(f"w_lo{k}", [P, HD], F32R) for k in range(3)]
        wo_sb = sb("wo_sb", [P, NP, D])
        gate_sb = sb("gate_sb", [P, E])
        gate_hi = sb("gate_hi", [P, E], F32R)
        gate_lo = sb("gate_lo", [P, E], F32R)
        brows = sb("brows", [2 * NP + E * FB, P])
        bcols = sb("bcols", [P, 2 * NP + E * FB])
        bv_all = sb("bv_all", [P, HD])
        bo_all = sb("bo_all", [P, D])
        b2_sb = sb("b2_sb", [E, D])
        rot = sb("rot", [P, 2, NC])
        mask = sb("mask", [P, 2 * P])
        ident = sb("ident", [P, P])
        iota = sb("iota", [P, E])
        neg_half = sb("neg_half", [P, NC])
        mv = sb("mv", [P, NC, 2])
        st6 = sb("st6", [P, NC, 6])
        rstd = sb("rstd", [P, NC])
        veps = sb("veps", [P, NC])
        xh = sb("xh", [P, SC, D])
        xT_hi = sb("xT_hi", [P, ST], F32R)
        xT_lo = sb("xT_lo", [P, ST], F32R)
        qT = sb("qT", [P, NP, ST])
        kT = sb("kT", [P, NP, ST])
        kn = sb("kn", [P, SC, HD])
        w_in = [kn[:, k, :] for k in range(3)]
        vb = sb("vb", [P, 2, HD // 2])
        vcs = sb("vcs", [P, SC, H, 2, VW])
        cs4 = sb("cs4", [P, 2, SC])
        am = sb("am", [P, 2, 2, 2 * P])
        state = sb("state", [P, NP, CS])
        tc = sb("tc", [P, 2, 2, GH // 2, VW])
        tcs = sb("tcs", [P, 2, H, VW])
        rden = sb("rden", [P, 2, H])
        dmax = sb("dmax", [P, 2, H])
        on = sb("on", [P, 2, H, DH])
        oT = sb("oT", [P, 2, NP, P])
        x2 = sb("x2", [P, SC, D])
        mv2 = sb("mv2", [P, SC, 2])
        st62 = sb("st62", [P, SC, 6])
        rstd2 = sb("rstd2", [P, SC])
        veps2 = sb("veps2", [P, SC])
        yh = sb("yh", [P, SC, D])
        yT_hi = sb("yT_hi", [P, ST], F32R)
        yT_lo = sb("yT_lo", [P, ST], F32R)
        yTall = sb("yTall", [P, 2, T], F32R)
        lg = sb("lg", [P, SC, E])
        top = sb("top", [P, SC, E])
        idx = sb("idx", [P, SC, E], U32)
        idxf = sb("idxf", [P, SC, 2])
        holder = sb("holder", [P, 1])
        gap = sb("gap", [P, SC])
        th = sb("th", [P, SC])
        wts = sb("wts", [P, 2, SC])
        hot = sb("hot", [P, SC, E])
        comb = sb("comb", [P, SC, E])
        comb_all = sb("comb_all", [P, NC, E])
        combT = sb("combT", [E, SC, P])
        w1_in = sb("w1_in", [P, EJ, F])
        w1_hi = w_hi[0][:].rearrange("p (j f) -> p j f", j=EJ)
        w1_lo = w_lo[0][:].rearrange("p (j f) -> p j f", j=EJ)
        b1_now = sb("b1_now", [P, EJ * FB])
        w2_sb = sb("w2_sb", [P, EJ, FB, D])
        hT = qT[:].rearrange("p (a b) t -> p a b t", a=2)
        acc = x_sb

        x_in = [sem(f"x_in{k}") for k in range(NS)]
        c_in = sem("c_in")
        wl_in = [sem(f"wl_in{k}") for k in range(3)]
        brow_in = sem("brow_in")
        memsets = sem("memsets")
        bT_ps = sem("bT_ps")
        bT_ok = sem("bT_ok")
        whi_ok = sem("whi_ok")
        wlo_ok = sem("wlo_ok")
        var1 = sem("var1")
        rstd1_ok = sem("rstd1_ok")
        dve_step = sem("dve_step")
        xh_ok = sem("xh_ok")
        xT_ps = sem("xT_ps")
        xThi_ok = sem("xThi_ok")
        xTlo_ok = sem("xTlo_ok")
        big_ps = sem("big_ps")
        big_ok = sem("big_ok")
        v_ps = sem("v_ps")
        v_add = sem("v_add")
        v_cos = sem("v_cos")
        v_sin = sem("v_sin")
        cs_ok = sem("cs_ok")
        vone = sem("vone")
        sc_ps = sem("sc_ps")
        am_ok = sem("am_ok")
        o_ps = sem("o_ps")
        tc_ok = sem("tc_ok")
        tcs_ok = sem("tcs_ok")
        st_ok = sem("st_ok")
        rden_ok = sem("rden_ok")
        on_ok = sem("on_ok")
        oT_ps = sem("oT_ps")
        oT_ok = sem("oT_ok")
        wo_ps = sem("wo_ps")
        x2_ok = sem("x2_ok")
        var2 = sem("var2")
        rstd2_ok = sem("rstd2_ok")
        yh_ok = sem("yh_ok")
        yT_ps = sem("yT_ps")
        yThi_ok = sem("yThi_ok")
        yTlo_ok = sem("yTlo_ok")
        yT_all = sem("yT_all")
        lg_ps = sem("lg_ps")
        gap_ok = sem("gap_ok")
        th_ok = sem("th_ok")
        comb_ok = sem("comb_ok")
        cT_ps = sem("cT_ps")
        cT_ok = sem("cT_ok")
        b2_ps = sem("b2_ps")
        acc0_ok = sem("acc0_ok")
        w1_load = [sem(f"w1_load{j}") for j in range(EJ)]
        w2_load = [sem(f"w2_load{j}") for j in range(EJ)]
        w1hi_ok = sem("w1hi_ok")
        w1lo_ok = sem("w1lo_ok")
        b1_ok = sem("b1_ok")
        h_ps = sem("h_ps")
        h_ok = sem("h_ok")
        y_ps = sem("y_ps")
        y_ok = sem("y_ok")
        stored = sem("stored")

        block = ctx.enter_context(nc.Block())
        f32 = lambda ap: ap.bitcast(F32)

        @block.sync
        def _(sp):
            xv = x.rearrange("a (c p) d -> p (a c) d", p=P)
            sp.dma_start(x_sb[:, 0:SC, :], xv[:, 0:SC, :]).then_inc(x_in[0], 16)
            sp.dma_start(w_in[0], Wq).then_inc(wl_in[0], 16)
            sp.dma_start(w_in[1], Wk).then_inc(wl_in[1], 16)
            sp.dma_start(w_in[2], Wv).then_inc(wl_in[2], 16)
            for k in range(1, NS):
                sp.dma_start(x_sb[:, k * SC:(k + 1) * SC, :], xv[:, k * SC:(k + 1) * SC, :]).then_inc(x_in[k], 16)
            sp.dma_start(wo_sb[:], Wo.rearrange("(b p) n -> p b n", p=P)).then_inc(c_in, 16)
            for j in range(EJ):
                sp.dma_start(w1_in[:, j, :], w1[j]).then_inc(w1_load[j], 16)
                sp.dma_start(w2_sb[:, j, :, :], w2[j].rearrange("(b p) d -> p b d", p=P)).then_inc(w2_load[j], 16)
            with sp.Fori(1, E // EJ) as i:
                for j in range(EJ):
                    sp.wait_ge(w1hi_ok, i * EJ + (j + 1 - EJ))
                    sp.wait_ge(w1lo_ok, i * EJ + (j + 1 - EJ))
                    sp.dma_start(w1_in[:, j, :], w1[bass.ds(i * EJ + j, 1), :, :].rearrange("e d f -> d (e f)")
                                 ).then_inc(w1_load[j], 16)
                    sp.wait_ge(y_ps, i * STEPS + (j + 1 - EJ) * NS)
                    sp.dma_start(w2_sb[:, j, :, :], w2[bass.ds(i * EJ + j, 1), :, :].rearrange("e (b p) d -> p (e b) d", p=P)
                                 ).then_inc(w2_load[j], 16)
            ov = out.rearrange("a (c p) d -> p (a c) d", p=P)
            for k in range(NS):
                sp.wait_ge(y_ok, E * NS - NS + k + 1)
                sp.dma_start(ov[:, k * SC:(k + 1) * SC, :], acc[:, k * SC:(k + 1) * SC, :]).then_inc(stored, 16)
            sp.wait_ge(stored, 16 * NS)

        @block.gpsimd
        def _(pool):
            pool.memset(neg_half[:], -0.5).then_inc(memsets, 1)
            pool.memset(state[:], 0.0).then_inc(memsets, 1)
            pool.wait_ge(memsets, 2)
            for k in range(NS):
                pool.wait_ge(var1, k + 1)
                pool.tensor_tensor(rstd[:, k * SC:(k + 1) * SC], veps[:, k * SC:(k + 1) * SC],
                                   neg_half[:, 0:SC], ALU.pow).then_inc(rstd1_ok, 1)
            with pool.Fori(0, NS) as i:
                for c in range(SC):
                    pool.wait_ge(rden_ok, i * SC + c + 1)
                    if c >= 2:
                        pool.wait_ge(oT_ps, i * 2 * SC + 2 * (c - 1))
                    pool.tensor_tensor(on[:, c % 2, :, :], tcs[:, c % 2, :, 0:DH],
                                       rden[:, c % 2, :, None].broadcast_to([P, H, DH]), ALU.mult
                                       ).then_inc(on_ok, 1)
                pool.wait_ge(var2, i + 1)
                pool.tensor_tensor(rstd2[:], veps2[:], neg_half[:, 0:SC], ALU.pow).then_inc(rstd2_ok, 1)
                pool.wait_ge(yThi_ok, i + 1)
                pool.tensor_copy(yTall[:, 0, bass.ds(i * ST, ST)], f32(yT_hi[:])).then_inc(yT_all, 1)
                pool.wait_ge(yTlo_ok, i + 1)
                pool.tensor_copy(yTall[:, 1, bass.ds(i * ST, ST)], f32(yT_lo[:])).then_inc(yT_all, 1)

        @block.scalar
        def _(act):
            act.dma_start(brows[0:NP, :], bq.rearrange("(r p) -> r p", p=P)).then_inc(brow_in, 16)
            act.dma_start(brows[NP:2 * NP, :], bk.rearrange("(r p) -> r p", p=P)).then_inc(brow_in, 16)
            act.dma_start(brows[2 * NP:, :], b1.rearrange("e (b p) -> (e b) p", p=P)).then_inc(brow_in, 16)
            act.dma_start(ident[:], c_ident).then_inc(brow_in, 16)
            act.dma_start(rot[:], c_rot.rearrange("p (a c) -> p a c", a=2)).then_inc(c_in, 16)
            act.dma_start(mask[:], c_mask).then_inc(c_in, 16)
            act.dma_start(bv_all[:], bv.rearrange("(a n) -> a n", a=1).broadcast_to([P, HD])).then_inc(c_in, 16)
            act.dma_start(bo_all[:], bo.rearrange("(a n) -> a n", a=1).broadcast_to([P, D])).then_inc(c_in, 16)
            act.dma_start(gate_sb[:], gate_w).then_inc(c_in, 16)
            act.dma_start(b2_sb[:], b2).then_inc(c_in, 16)
            act.dma_start(iota[:], c_iota).then_inc(c_in, 16)
            for k in range(3):
                act.wait_ge(wl_in[k], 16)
                act.activation(w_hi[k][:], w_in[k], ACT.Copy).then_inc(whi_ok, 1)
            act.wait_ge(bT_ps, 1)
            act.activation(bcols[:], ps[:, 6, 0:2 * NP + E * FB], ACT.Copy).then_inc(bT_ok, 1)
            act.wait_ge(c_in, 16 * 8)
            act.activation(gate_hi[:], gate_sb[:], ACT.Copy).then_inc(whi_ok, 1)
            act.wait_ge(bT_ok, 1)
            with act.Fori(0, NS) as i:
                act.wait_ge(xT_ps, i + 1)
                act.activation(xT_hi[:], ps[:, 7, :], ACT.Copy).then_inc(xThi_ok, 1)
                for j in range(QK_JOBS):
                    act.wait_ge(big_ps, i * BIG_JOBS + j + 1)
                    dst = (kT if j < NP else qT)[:, j % NP, :]
                    col = (NP if j < NP else 0) + j % NP
                    act.activation(dst, ps[:, j % 4, :], ACT.Relu, bias=bcols[:, col:col + 1]).then_inc(big_ok, 1)
                for m in range(KN_JOBS):
                    act.wait_ge(big_ps, i * BIG_JOBS + QK_JOBS + m + 1)
                    act.activation(kn[:, m // 2, (m % 2) * 512:(m % 2) * 512 + 512], ps[:, (QK_JOBS + m) % 4, :],
                                   ACT.Copy).then_inc(big_ok, 1)
                    act.wait_ge(v_add, i * V_JOBS + m + 1)
                    if m == 0:
                        act.wait_ge(cs_ok, i + 1)
                    act.activation(vcs[:, m // 2, (m % 2) * 8:(m % 2) * 8 + 8, 0, 0:DH],
                                   vb[:, m % 2, :].rearrange("p (h d) -> p h d", d=DH), ACT.Copy,
                                   scale=cs4[:, 0, m // 2:m // 2 + 1]).then_inc(v_cos, 1)
                def turn_out(c):
                    for half in range(2):
                        act.wait_ge(oT_ps, i * 2 * SC + 2 * c + half + 1)
                        act.activation(oT[:, c % 2, half * 4:half * 4 + 4, :],
                                       ps[:, 6 + half, :].rearrange("p (a b) -> p a b", b=P), ACT.Copy
                                       ).then_inc(oT_ok, 1)

                for n in range(GROUPS):
                    c, g = n // NG, n % NG
                    act.wait_ge(o_ps, i * GROUPS + n + 1)
                    if n >= 2:
                        act.wait_ge(tcs_ok, i * GROUPS + n - 1)
                    act.activation(tc[:, n % 2, :, :, :],
                                   ps[:, 2 + 2 * (n % 2):4 + 2 * (n % 2), 0:2 * CS]
                                   .rearrange("p a (b s v) -> p a b s v", b=2, s=2)[:, :, :, 0, :],
                                   ACT.Copy, scale=cs4[:, 0, c:c + 1]).then_inc(tc_ok, 1)
                    if g == 2 and c >= 1:
                        turn_out(c - 1)
                turn_out(SC - 1)
                act.wait_ge(yT_ps, i + 1)
                act.activation(yT_hi[:], ps[:, 6, :], ACT.Copy).then_inc(yThi_ok, 1)
                act.wait_ge(gap_ok, i + 1)
                act.activation(th[:], gap[:], ACT.Tanh, scale=0.5).then_inc(th_ok, 1)
                act.wait_ge(cT_ps, i + 1)
                act.activation(combT[:], ps[0:E, 7, :].rearrange("p (a b) -> p a b", b=P), ACT.Copy).then_inc(cT_ok, 1)
            with act.Fori(0, E // EJ) as i:
                act.activation(b1_now[:], bcols[:, bass.ds(i * EJ * FB + 2 * NP, EJ * FB)], ACT.Copy).then_inc(b1_ok, 1)
                act.wait_ge(b1_ok, i + 1)
                for j in range(EJ):
                    act.wait_ge(w1_load[j], i * 16 + 16)
                    act.activation(w1_hi[:, j, :], w1_in[:, j, :], ACT.Copy).then_inc(w1hi_ok, 1)
                for n in range(STEPS):
                    j = n // NS
                    if n >= 2:
                        act.wait_ge(y_ps, i * STEPS + n - 1)
                    for b in range(FB):
                        act.wait_ge(h_ps, (i * STEPS + n) * FB + b + 1)
                        bank = (n * FB + b) % 4
                        act.activation(hT[:, n % 2, b, :], ps[:, bank, :], ACT.Gelu,
                                       bias=b1_now[:, j * FB + b:j * FB + b + 1]).then_inc(h_ok, 1)
                act.wait_ge(h_ok, i * STEPS * FB + STEPS * FB)

        @block.vector
        def _(dve):
            steps = [0]

            def link(ins):
                steps[0] += 1
                ins.then_inc(dve_step, 1)
                dve.wait_ge(dve_step, steps[0])

            for k in range(NS):
                dve.wait_ge(x_in[k], 16)
                for c in range(k * SC, (k + 1) * SC):
                    last = dve.bn_stats(st6[:, c, :], x_sb[:, c, :])
                link(last)
                for c in range(k * SC, (k + 1) * SC):
                    last = dve.bn_aggr(mv[:, c, :], st6[:, c, :])
                link(last)
                dve.tensor_scalar(veps[:, k * SC:(k + 1) * SC], mv[:, k * SC:(k + 1) * SC, 1], EPS, None, ALU.add
                                  ).then_inc(var1, 1)
                if k < 3:
                    dve.wait_ge(whi_ok, k + 1)
                    dve.tensor_tensor(w_lo[k][:], w_in[k], f32(w_hi[k][:]), ALU.subtract).then_inc(wlo_ok, 1)
            dve.wait_ge(whi_ok, 4)
            dve.tensor_tensor(gate_lo[:], gate_sb[:], f32(gate_hi[:]), ALU.subtract).then_inc(wlo_ok, 1)
            dve.wait_ge(rstd1_ok, NS)
            dve.wait_ge(memsets, 2)
            base = steps[0]
            per = 0

            with dve.Fori(0, NS) as i:
                inner = [0]
                PER = 12

                def chain(ins):
                    inner[0] += 1
                    ins.then_inc(dve_step, 1)
                    dve.wait_ge(dve_step, i * PER + base + inner[0])

                for c in range(SC):
                    dve.tensor_scalar(xh[:, c, :], x_sb[:, bass.ds(i * SC + c, 1), :].rearrange("p a d -> p (a d)"),
                                      mv[:, bass.ds(i * SC + c, 1), 0], rstd[:, bass.ds(i * SC + c, 1)],
                                      ALU.subtract, ALU.mult).then_inc(xh_ok, 1)
                dve.tensor_copy(cs4[:], rot[:, :, bass.ds(i * SC, SC)]).then_inc(cs_ok, 1)
                dve.wait_ge(xT_ps, i + 1)
                dve.wait_ge(xThi_ok, i + 1)
                dve.tensor_tensor(xT_lo[:], ps[:, 7, :], f32(xT_hi[:]), ALU.subtract).then_inc(xTlo_ok, 1)
                dve.wait_ge(cs_ok, i + 1)
                for c in range(SC):
                    for s in range(2):
                        last = dve.tensor_copy(vcs[:, c, :, s, DH], cs4[:, s, c:c + 1].broadcast_to([P, H]))
                last.then_inc(vone, 1)
                for m in range(V_JOBS):
                    dve.wait_ge(v_ps, i * V_JOBS + m + 1)
                    if m >= 2:
                        dve.wait_ge(v_cos, i * V_JOBS + m - 1)
                        dve.wait_ge(v_sin, i * V_JOBS + m - 1)
                    dve.tensor_tensor(vb[:, m % 2, :], ps[:, 4 + m % 2, :], bv_all[:, (m % 2) * 512:(m % 2) * 512 + 512],
                                      ALU.add).then_inc(v_add, 1)
                    dve.wait_ge(v_add, i * V_JOBS + m + 1)
                    dve.tensor_scalar(vcs[:, m // 2, (m % 2) * 8:(m % 2) * 8 + 8, 1, 0:DH],
                                      vb[:, m % 2, :].rearrange("p (h d) -> p h d", d=DH),
                                      cs4[:, 1, m // 2:m // 2 + 1], None, ALU.mult).then_inc(v_sin, 1)

                def masked(n):
                    dve.wait_ge(sc_ps, i * GROUPS + n + 1)
                    if n >= 2:
                        dve.wait_ge(o_ps, i * GROUPS + n - 1)
                    dve.tensor_tensor(am[:, n % 2, :, :], ps[:, 0:2, 0:2 * P],
                                      mask[:, None, :].broadcast_to([P, 2, 2 * P]), ALU.mult).then_inc(am_ok, 1)

                def taken(n):
                    c, g = n // NG, n % NG
                    ob = ps[:, 2 + 2 * (n % 2):4 + 2 * (n % 2), :]
                    if g == 0 and c >= 2:
                        dve.wait_ge(on_ok, i * SC + c - 1)
                    dve.wait_ge(tc_ok, i * GROUPS + n + 1)
                    dve.tensor_tensor(state[:, 2 * g:2 * g + 2, :], ob[:, :, 2 * CS:3 * CS],
                                      state[:, 2 * g:2 * g + 2, :], ALU.add).then_inc(st_ok, 1)
                    for r in range(2):
                        last = dve.scalar_tensor_tensor(
                            out=tcs[:, c % 2, g * GH + r:(g + 1) * GH:2, :],
                            in0=ob[:, r, 0:2 * CS].rearrange("p (b s v) -> p b s v", b=2, s=2)[:, :, 1, :],
                            scalar=cs4[:, 1, c:c + 1], in1=tc[:, n % 2, r, :, :],
                            op0=ALU.mult, op1=ALU.add)
                    last.then_inc(tcs_ok, 1)
                    if g == NG - 1:
                        dve.wait_ge(tcs_ok, i * GROUPS + n + 1)
                        chain(dve.tensor_scalar(dmax[:, c % 2, :], tcs[:, c % 2, :, DH], DEN_MIN, None, ALU.max))
                        dve.reciprocal(rden[:, c % 2, :], dmax[:, c % 2, :]).then_inc(rden_ok, 1)

                def residual(c):
                    dve.wait_ge(wo_ps, i * SC + c + 1)
                    dve.tensor_tensor(x2[:, c, :], ps[:, 7, 0:D], x2[:, c, :], ALU.add).then_inc(x2_ok, 1)

                chain(dve.tensor_tensor(x2[:], x_sb[:, bass.ds(i * SC, SC), :],
                                        bo_all[:, None, :].broadcast_to([P, SC, D]), ALU.add))
                for n in range(GROUPS + 1):
                    if n < GROUPS:
                        masked(n)
                    if n >= 1:
                        taken(n - 1)
                    if n % NG == 3 and n >= NG:
                        residual(n // NG - 1)
                residual(SC - 1)
                dve.wait_ge(x2_ok, i * SC + SC)
                for c in range(SC):
                    last = dve.bn_stats(st62[:, c, :], x2[:, c, :])
                chain(last)
                dve.memset(holder[:], 0.0)
                for c in range(SC):
                    last = dve.bn_aggr(mv2[:, c, :], st62[:, c, :])
                chain(last)
                dve.tensor_scalar(veps2[:], mv2[:, :, 1], EPS, None, ALU.add).then_inc(var2, 1)
                dve.wait_ge(rstd2_ok, i + 1)
                for c in range(SC):
                    last = dve.tensor_scalar(yh[:, c, :], x2[:, c, :], mv2[:, c, 0:1], rstd2[:, c:c + 1],
                                             ALU.subtract, ALU.mult)
                last.then_inc(yh_ok, 1)
                dve.wait_ge(yT_ps, i + 1)
                dve.wait_ge(yThi_ok, i + 1)
                dve.tensor_tensor(yT_lo[:], ps[:, 6, :], f32(yT_hi[:]), ALU.subtract).then_inc(yTlo_ok, 1)
                dve.wait_ge(lg_ps, i + 1)
                chain(dve.tensor_copy(lg[:], ps[:, 7, 0:SC * E].rearrange("p (c e) -> p c e", e=E)))
                dve.memset(holder[:], 0.0)
                for c in range(SC):
                    last = dve.max(top[:, c, :], lg[:, c, :])
                chain(last)
                dve.tensor_tensor(gap[:], top[:, :, 0], top[:, :, 1], ALU.subtract).then_inc(gap_ok, 1)
                for c in range(SC):
                    last = dve.max_index(idx[:, c, :], top[:, c, :], lg[:, c, :])
                chain(last)
                dve.tensor_copy(idxf[:], idx[:, :, 0:2])
                dve.wait_ge(th_ok, i + 1)
                dve.tensor_scalar(wts[:, 0, :], th[:], 0.5, 0.5, ALU.mult, ALU.add)
                chain(dve.tensor_scalar(wts[:, 1, :], th[:], -0.5, 0.5, ALU.mult, ALU.add))
                for c in range(SC):
                    last = dve.tensor_scalar(hot[:, c, :], iota[:], idxf[:, c, 1:2], wts[:, 1, c:c + 1],
                                             ALU.is_equal, ALU.mult)
                    last = dve.tensor_scalar(comb[:, c, :], iota[:], idxf[:, c, 0:1], wts[:, 0, c:c + 1],
                                             ALU.is_equal, ALU.mult)
                chain(last)
                dve.tensor_tensor(comb[:], comb[:], hot[:], ALU.add).then_inc(comb_ok, 1)
                dve.wait_ge(comb_ok, i + 1)
                dve.tensor_copy(comb_all[:, bass.ds(i * SC, SC), :], comb[:])
                dve.wait_ge(b2_ps, i + 1)
                dve.tensor_tensor(acc[:, bass.ds(i * SC, SC), :], ps[:, 6, :].rearrange("p (c d) -> p c d", d=D),
                                  x2[:], ALU.add).then_inc(acc0_ok, 1)
                assert inner[0] == PER, inner[0]
            dve.wait_ge(acc0_ok, NS)
            with dve.Fori(0, E // EJ) as i:
                for j in range(EJ):
                    dve.wait_ge(w1hi_ok, i * EJ + j + 1)
                    dve.tensor_tensor(w1_lo[:, j, :], w1_in[:, j, :], f32(w1_hi[:, j, :]), ALU.subtract
                                      ).then_inc(w1lo_ok, 1)
                for n in range(STEPS):
                    j, s = n // NS, n % NS
                    dve.wait_ge(y_ps, i * STEPS + n + 1)
                    for c in range(SC):
                        k = s * SC + c
                        last = dve.scalar_tensor_tensor(
                            out=acc[:, k, :], in0=ps[:, 6 + n % 2, c * D:(c + 1) * D],
                            scalar=comb_all[:, k, bass.ds(i * EJ + j, 1)], in1=acc[:, k, :],
                            op0=ALU.mult, op1=ALU.add)
                    last.then_inc(y_ok, 1)

        @block.tensor
        def _(pe):
            mm = pe.matmul
            pe.wait_ge(brow_in, 16 * 4)
            pe.transpose(ps[:, 6, 0:2 * NP + E * FB], brows[:], ident[0:2 * NP + E * FB, 0:2 * NP + E * FB]
                         ).then_inc(bT_ps, 1)
            pe.wait_ge(bT_ok, 1)
            pe.wait_ge(c_in, 16 * 8)

            def split3(o, a, b, part_a, part_b):
                mm(o, part_a(a[0]), part_b(b[0]), start=True, stop=False)
                mm(o, part_a(a[0]), part_b(b[1]), start=False, stop=False)
                return mm(o, part_a(a[1]), part_b(b[0]), start=False, stop=True)

            with pe.Fori(0, NS) as i:
                for c in range(SC):
                    pe.wait_ge(xh_ok, i * SC + c + 1)
                    last = pe.transpose(ps[:, 7, c * P:(c + 1) * P], xh[:, c, :], ident[:])
                last.then_inc(xT_ps, 1)
                pe.wait_ge(xThi_ok, i + 1)
                pe.wait_ge(xTlo_ok, i + 1)
                for j in range(QK_JOBS):
                    w = 1 if j < NP else 0
                    if j == 0:
                        pe.wait_ge(whi_ok, 4)
                        pe.wait_ge(wlo_ok, 4)
                    if j >= 4:
                        pe.wait_ge(big_ok, i * BIG_JOBS + j - 3)
                    b = j % NP
                    split3(ps[:, j % 4, :], (w_hi[w], w_lo[w]), (xT_hi, xT_lo),
                           lambda t: t[:, b * P:(b + 1) * P], lambda t: t[:]).then_inc(big_ps, 1)
                for m in range(V_JOBS):
                    c, half = m // 2, m % 2
                    if m >= 2:
                        pe.wait_ge(v_add, i * V_JOBS + m - 1)
                    split3(ps[:, 4 + m % 2, :], (xT_hi, xT_lo), (w_hi[2], w_lo[2]),
                           lambda t: t[:, c * P:(c + 1) * P], lambda t: t[:, half * 512:half * 512 + 512]
                           ).then_inc(v_ps, 1)
                    j = QK_JOBS + m
                    pe.wait_ge(big_ok, i * BIG_JOBS + j - 3)
                    for q in range(4):
                        last = pe.transpose(ps[:, j % 4, q * P:(q + 1) * P],
                                            kT[:, half * 4 + q, c * P:(c + 1) * P], ident[:])
                    last.then_inc(big_ps, 1)
                pe.wait_ge(big_ok, i * BIG_JOBS + BIG_JOBS)
                pe.wait_ge(v_add, i * V_JOBS + V_JOBS)

                def scores(n):
                    c, g = n // NG, n % NG
                    if n >= 1:
                        pe.wait_ge(am_ok, i * GROUPS + n)
                    for h in range(g * GH, (g + 1) * GH):
                        r = slice(64 * (h % 2), 64 * (h % 2) + 64)
                        col = (h % GH) // 2 * P
                        last = mm(ps[:, h % 2, col:col + P], kT[r, h // 2, c * P:(c + 1) * P],
                                  qT[r, h // 2, c * P:(c + 1) * P], start=True, stop=True)
                    last.then_inc(sc_ps, 1)

                def outputs(n):
                    c, g = n // NG, n % NG
                    pe.wait_ge(am_ok, i * GROUPS + n + 1)
                    if n >= 2:
                        pe.wait_ge(tcs_ok, i * GROUPS + n - 1)
                        pe.wait_ge(st_ok, i * GROUPS + n - 1)
                    if c >= 1:
                        pe.wait_ge(st_ok, i * GROUPS + n - NG + 1)
                    if g == 0:
                        pe.wait_ge(v_cos, i * V_JOBS + 2 * c + 2)
                        pe.wait_ge(v_sin, i * V_JOBS + 2 * c + 2)
                        pe.wait_ge(vone, i + 1)
                    for h in range(g * GH, (g + 1) * GH):
                        q, r = h % GH // 2, h % 2
                        mm(ps[:, 2 + 2 * (n % 2) + r, q * CS:(q + 1) * CS], am[:, n % 2, r, q * P:(q + 1) * P],
                           vcs[:, c, h, :, :].rearrange("p s v -> p (s v)"), start=(q == 0), stop=False,
                           skip_group_check=True)
                    for h in range(g * GH, (g + 1) * GH):
                        q, r = h % GH // 2, h % 2
                        rows = slice(64 * r, 64 * r + 64)
                        mm(ps[:, 2 + 2 * (n % 2) + r, q * CS:(q + 1) * CS], qT[rows, h // 2, c * P:(c + 1) * P],
                           state[rows, h // 2, :], start=False, stop=True, skip_group_check=True)
                    for h in range(g * GH, (g + 1) * GH):
                        q, r = h % GH // 2, h % 2
                        last = mm(ps[64 * r:64 * r + 64, 2 + 2 * (n % 2) + q, 2 * CS:3 * CS],
                                  kn[:, c, h * DH:(h + 1) * DH], vcs[:, c, h, :, :].rearrange("p s v -> p (s v)"),
                                  start=True, stop=True, skip_group_check=True)
                    last.then_inc(o_ps, 1)

                def turn_out(c):
                    pe.wait_ge(on_ok, i * SC + c + 1)
                    for half in range(2):
                        if half == 1 and c >= 1:
                            pe.wait_ge(x2_ok, i * SC + c)
                        for q in range(4):
                            pr = half * 4 + q
                            last = pe.transpose(ps[:, 6 + half, q * P:(q + 1) * P],
                                                on[:, c % 2, 2 * pr:2 * pr + 2, :].rearrange("p h d -> p (h d)"),
                                                ident[:])
                        last.then_inc(oT_ps, 1)

                def project(c):
                    pe.wait_ge(oT_ok, i * 2 * SC + 2 * c + 2)
                    for pr in range(NP):
                        last = mm(ps[:, 7, 0:D], oT[:, c % 2, pr, :], wo_sb[:, pr, :], start=(pr == 0), stop=(pr == NP - 1))
                    last.then_inc(wo_ps, 1)

                for n in range(GROUPS + 1):
                    if n < GROUPS:
                        scores(n)
                    if n >= 1:
                        outputs(n - 1)
                    if n % NG == 2 and n >= NG:
                        turn_out(n // NG - 1)
                    if n % NG == 3 and n >= NG:
                        project(n // NG - 1)
                turn_out(SC - 1)
                project(SC - 1)
                pe.wait_ge(yh_ok, i + 1)
                for c in range(SC):
                    last = pe.transpose(ps[:, 6, c * P:(c + 1) * P], yh[:, c, :], ident[:])
                last.then_inc(yT_ps, 1)
                pe.wait_ge(yThi_ok, i + 1)
                pe.wait_ge(yTlo_ok, i + 1)
                for c in range(SC):
                    last = split3(ps[:, 7, c * E:(c + 1) * E], (yT_hi, yT_lo), (gate_hi, gate_lo),
                                  lambda t: t[:, c * P:(c + 1) * P], lambda t: t[:])
                last.then_inc(lg_ps, 1)
                pe.wait_ge(comb_ok, i + 1)
                for c in range(SC):
                    last = pe.transpose(ps[0:E, 7, c * P:(c + 1) * P], comb[:, c, :], ident[:])
                last.then_inc(cT_ps, 1)
                pe.wait_ge(cT_ok, i + 1)
                for c in range(SC):
                    last = mm(ps[:, 6, c * D:(c + 1) * D], combT[:, c, :], b2_sb[:], start=True, stop=True)
                last.then_inc(b2_ps, 1)
            pe.wait_ge(acc0_ok, NS)
            pe.wait_ge(yT_all, 2 * NS)

            with pe.Fori(0, E // EJ) as i:
                def hidden(n):
                    j, s = n // NS, n % NS
                    if s == 0:
                        pe.wait_ge(w1lo_ok, i * EJ + j + 1)
                        pe.wait_ge(w1hi_ok, i * EJ + j + 1)
                    for b in range(FB):
                        k = n * FB + b
                        if k >= 4:
                            pe.wait_ge(h_ok, i * STEPS * FB + k - 3)
                        split3(ps[:, k % 4, :], (w1_hi, w1_lo), (0, 1),
                               lambda t: t[:, j, b * P:(b + 1) * P], lambda t: yTall[:, t, s * ST:(s + 1) * ST]
                               ).then_inc(h_ps, 1)

                def down(n):
                    j = n // NS
                    pe.wait_ge(h_ok, (i * STEPS + n + 1) * FB)
                    if n % NS == 0:
                        pe.wait_ge(w2_load[j], i * 16 + 16)
                    if n >= 2:
                        pe.wait_ge(y_ok, i * STEPS + n - 1)
                    for c in range(SC):
                        for b in range(FB):
                            last = mm(ps[:, 6 + n % 2, c * D:(c + 1) * D], hT[:, n % 2, b, c * P:(c + 1) * P],
                                      w2_sb[:, j, b, :], start=(b == 0), stop=(b == FB - 1))
                    last.then_inc(y_ps, 1)

                for n in range(STEPS + 1):
                    if n < STEPS:
                        hidden(n)
                    if n >= 1:
                        down(n - 1)
                pe.wait_ge(y_ok, i * STEPS + STEPS)


_INS = ["L0_attn_x", "L0_attn_Wq", "L0_attn_bq", "L0_attn_Wk", "L0_attn_bk", "L0_attn_Wv", "L0_attn_bv",
        "L0_attn_Wo", "L0_attn_bo", "L0_ffn_gate_w", "L0_ffn_w1", "L0_ffn_b1", "L0_ffn_w2", "L0_ffn_b2"]


def shape_constants():
    angles = np.float32(math.pi / (2.0 * T)) * np.arange(T, dtype=np.float32)
    rot = np.stack([np.cos(angles), np.sin(angles)]).astype(np.float32)
    rot = np.ascontiguousarray(rot.reshape(2, NC, P).transpose(2, 0, 1).reshape(P, 2 * NC))
    mask = np.tile(np.triu(np.ones((P, P), np.float32)), (1, 2))
    iota = np.tile(np.arange(E, dtype=np.float32), (P, 1))
    return {"c_rot": rot, "c_mask": mask, "c_ident": np.eye(P, dtype=np.float32), "c_iota": iota}


def kernel(**inputs):
    import concourse.bacc as bacc
    from concourse.bass_utils import run_bass_kernel_spmd

    nc = bacc.Bacc("TRN2", target_bir_lowering=False, num_devices=1)
    arrays = {f"in_{name}": np.ascontiguousarray(inputs[name]) for name in _INS}
    arrays.update(shape_constants())
    args = [nc.dram_tensor(n, a.shape, mybir.dt.from_np(a.dtype), kind="ExternalInput").ap()
            for n, a in arrays.items()]
    out = nc.dram_tensor("out", (1, T, D), F32, kind="ExternalOutput").ap()
    moe_block(nc, *args, out)
    r = run_bass_kernel_spmd(nc, [arrays], core_ids=[0])
    return r.results[0]["out"]
```

```python
import math
from contextlib import ExitStack

import numpy as np

import concourse.bass as bass
from concourse import mybir

ALU = mybir.AluOpType
ACT = mybir.ActivationFunctionType
F32 = mybir.dt.float32
F32R = mybir.dt.float32r
U32 = mybir.dt.uint32

P = 128
T, D = 2048, 128
H, DH = 16, 64
HD = H * DH
E, F = 8, 512
EPS = 1e-5
DEN_MIN = 1e-6
NC = T // P
SC = 4
NS = NC // SC
ST = SC * P
NP = H // 2
VW = DH + 1
CS = 2 * VW
GH = 4
NG = H // GH
FB = F // P
EJ = 2

QK_JOBS = 2 * NP
V_JOBS = 2 * SC
K_JOBS = 2 * SC
TOK_JOBS = V_JOBS + K_JOBS
GROUPS = SC * NG

TOK = [("k", 0)]
for _m in range(K_JOBS - 1):
    TOK += [("k", _m + 1), ("v", _m)]
TOK.append(("v", V_JOBS - 1))
OT_AT, WO_AT, YT_AT, GATE_AT = 2, 4, 11, 14
STATS_AFTER, NORM_AFTER, NORMED_AFTER, YLOW_AFTER = 3, 4, (6, 7), 10


STEPS = EJ * NS
AHEAD = 4


def step(n):
    return n % STEPS // NS, n % NS


def moe_block(nc, x, Wq, bq, Wk, bk, Wv, bv, Wo, bo, gate_w, w1, b1, w2, b2,
              c_rot, c_mask, c_ident, c_iota, out, rows):
    with ExitStack() as ctx:
        def sb(name, shape, dt=F32):
            return ctx.enter_context(nc.sbuf_tensor(name, shape, dt))

        def sem(name):
            return ctx.enter_context(nc.semaphore(name))

        ps = ctx.enter_context(nc.psum_tensor("ps", [P, 8, 512], F32))

        x_sb = sb("x_sb", [P, NC + SC, D])
        w_hi = [sb(f"w_hi{k}", [P, HD], F32R) for k in range(3)]
        w_lo = [sb(f"w_lo{k}", [P, HD], F32R) for k in range(3)]
        wo_sb = sb("wo_sb", [P, NP, D])
        gate_sb = sb("gate_sb", [P, E])
        gate_hi = sb("gate_hi", [P, E], F32R)
        gate_lo = sb("gate_lo", [P, E], F32R)
        brows = sb("brows", [2 * NP + E * FB, P])
        bcols = sb("bcols", [P, 2 * NP + E * FB])
        bv_all = sb("bv_all", [P, HD])
        bk_all = sb("bk_all", [P, HD])
        bo_all = sb("bo_all", [P, D])
        b2_sb = sb("b2_sb", [E, D])
        rot = sb("rot", [P, 2, NC])
        mask = sb("mask", [P, P])
        ident = sb("ident", [P, P])
        iota = sb("iota", [P, E])
        neg_half = sb("neg_half", [P, NC])
        mv = sb("mv", [P, NC + SC, 2])
        st6 = sb("st6", [P, NC, 6])
        rstd = sb("rstd", [P, NC + SC])
        veps = sb("veps", [P, NC])
        xh = sb("xh", [P, SC, D])
        xT_hi = sb("xT_hi", [P, ST], F32R)
        xT_lo = sb("xT_lo", [P, ST], F32R)
        attn = ExitStack()

        def sb_attn(name, shape):
            return attn.enter_context(nc.sbuf_tensor(name, shape, F32))

        cs4 = sb("cs4", [P, 2, SC])
        am = sb("am", [P, 2, 2, 2 * P])
        state = sb("state", [P, NP, CS])
        tc = sb("tc", [P, 2, 2, GH // 2, VW])
        tcs = sb("tcs", [P, 2, H, VW])
        rden = sb("rden", [P, 2, H])
        dmax = sb("dmax", [P, 2, H])
        on = sb("on", [P, 2, H, DH])
        oT = sb("oT", [P, 2, NP, P])
        x2 = sb("x2", [P, SC, D])
        mv2 = sb("mv2", [P, SC, 2])
        st62 = sb("st62", [P, SC, 6])
        rstd2 = sb("rstd2", [P, SC])
        veps2 = sb("veps2", [P, SC])
        yh = xh
        yT_hi = sb("yT_hi", [P, ST], F32R)
        yT_lo = sb("yT_lo", [P, ST], F32R)
        yTall = sb("yTall", [P, 2, T], F32R)
        lg = sb("lg", [P, SC, E])
        top = sb("top", [P, SC, E])
        idx = sb("idx", [P, SC, E], U32)
        idxf = sb("idxf", [P, SC, 2])
        warm = sb("warm", [P, 1])
        holder = sb("holder", [P, 1])
        gap = sb("gap", [P, SC])
        th = sb("th", [P, SC])
        wts = sb("wts", [P, 2, SC])
        hot = sb("hot", [P, 2, SC, E])
        comb = sb("comb", [P, SC, E])
        combT = sb("combT", [E, SC, P])
        w1_in = sb("w1_in", [P, EJ, F])
        w1_hi = w_hi[0][:].rearrange("p (j f) -> p j f", j=EJ)
        w1_lo = w_lo[0][:].rearrange("p (j f) -> p j f", j=EJ)
        b1_now = sb("b1_now", [P, EJ * FB])
        w2_in = sb("w2_in", [P, EJ, FB, D])
        acc = x_sb
        qT = sb_attn("qT", [P, NP, ST])
        kT = sb_attn("kT", [P, NP, ST])
        kn = sb_attn("kn", [P, SC, HD])
        w_in = [kn[:, k, :] for k in (3, 1, 2)]
        vb = sb_attn("vb", [P, 2, HD // 2])
        vcs = sb_attn("vcs", [P, SC, H, 2, VW])
        attn.close()
        hT = sb("hT", [P, FB, ST])
        hT_hi = sb("hT_hi", [P, 2, FB, ST], F32R)
        hT_lo = sb("hT_lo", [P, 2, FB, ST], F32R)
        w2_hi = sb("w2_hi", [P, EJ, FB, D], F32R)
        w2_lo = sb("w2_lo", [P, EJ, FB, D], F32R)
        comb_row = sb("comb_row", [P, EJ, T])
        part = sb("part", [P, 2, ST])
        accT = sb("accT", [P, T])

        x_in = [sem(f"x_in{k}") for k in range(NS)]
        c_in = sem("c_in")
        wl_in = [sem(f"wl_in{k}") for k in range(3)]
        brow_in = sem("brow_in")
        memsets = sem("memsets")
        bT_ps = sem("bT_ps")
        bT_ok = sem("bT_ok")
        whi_ok = sem("whi_ok")
        wlo_ok = sem("wlo_ok")
        var1 = sem("var1")
        rstd1_ok = sem("rstd1_ok")
        bn1_ok = sem("bn1_ok")
        mv1_ok = sem("mv1_ok")
        x2_open = sem("x2_open")
        dmax_ok = sem("dmax_ok")
        bn2_ok = sem("bn2_ok")
        mv2_ok = sem("mv2_ok")
        lg_ok = sem("lg_ok")
        top_ok = sem("top_ok")
        idx_ok = sem("idx_ok")
        idxf_ok = sem("idxf_ok")
        wts_ok = sem("wts_ok")
        hot_ok = sem("hot_ok")
        hotw_ok = sem("hotw_ok")
        xh_ok = sem("xh_ok")
        xT_ps = sem("xT_ps")
        xThi_ok = sem("xThi_ok")
        xTlo_ok = sem("xTlo_ok")
        big_ps = sem("big_ps")
        big_ok = sem("big_ok")
        row_in = sem("row_in")
        tok_ps = sem("tok_ps")
        tok_ok = sem("tok_ok")
        kn_ok = sem("kn_ok")
        v_rot = sem("v_rot")
        cs_ok = sem("cs_ok")
        vone = sem("vone")
        sc_ps = sem("sc_ps")
        am_ok = sem("am_ok")
        o_ps = sem("o_ps")
        tc_ok = sem("tc_ok")
        tcs_ok = sem("tcs_ok")
        st_ok = sem("st_ok")
        rden_ok = sem("rden_ok")
        on_ok = sem("on_ok")
        oT_ps = sem("oT_ps")
        oT_ok = sem("oT_ok")
        wo_ps = sem("wo_ps")
        x2_ok = sem("x2_ok")
        var2 = sem("var2")
        rstd2_ok = sem("rstd2_ok")
        yh_ok = sem("yh_ok")
        yT_ps = sem("yT_ps")
        yThi_ok = sem("yThi_ok")
        yTlo_ok = sem("yTlo_ok")
        yT_all = sem("yT_all")
        lg_ps = sem("lg_ps")
        gap_ok = sem("gap_ok")
        th_ok = sem("th_ok")
        comb_ok = sem("comb_ok")
        cT_ps = sem("cT_ps")
        cT_ok = sem("cT_ok")
        b2_ps = sem("b2_ps")
        acc0_ok = sem("acc0_ok")
        w1_load = [sem(f"w1_load{j}") for j in range(EJ)]
        w2_load = [sem(f"w2_load{j}") for j in range(EJ)]
        comb_out = sem("comb_out")
        comb_early = sem("comb_early")
        comb_load = [sem(f"comb_load{j}") for j in range(EJ)]
        w2hi_ok = sem("w2hi_ok")
        w2lo_ok = sem("w2lo_ok")
        w1hi_ok = sem("w1hi_ok")
        w1lo_ok = sem("w1lo_ok")
        b1_ok = sem("b1_ok")
        h_ps = sem("h_ps")
        h_ok = sem("h_ok")
        hhi_ok = sem("hhi_ok")
        hlo_ok = sem("hlo_ok")
        y_ps = sem("y_ps")
        part_ok = sem("part_ok")
        accT_zero = sem("accT_zero")
        accT_ok = sem("accT_ok")
        accT_end = sem("accT_end")
        back_ps = sem("back_ps")
        out_ok = sem("out_ok")
        stored = sem("stored")

        block = ctx.enter_context(nc.Block())
        f32 = lambda ap: ap.bitcast(F32)

        @block.sync
        def _(sp):
            xv = x.rearrange("a (c p) d -> p (a c) d", p=P)
            sp.dma_start(x_sb[:, 0:SC, :], xv[:, 0:SC, :]).then_inc(x_in[0], 16)
            sp.dma_start(w_in[1], Wk).then_inc(wl_in[1], 16)
            sp.dma_start(ident[:], c_ident).then_inc(brow_in, 16)
            sp.dma_start(w_in[2], Wv).then_inc(wl_in[2], 16)
            sp.dma_start(bk_all[:], bk.rearrange("(a n) -> a n", a=1).broadcast_to([P, HD])).then_inc(row_in, 16)
            sp.dma_start(rot[:], c_rot.rearrange("p (a c) -> p a c", a=2)).then_inc(row_in, 16)
            sp.dma_start(bv_all[:], bv.rearrange("(a n) -> a n", a=1).broadcast_to([P, HD])).then_inc(row_in, 16)
            sp.dma_start(gate_sb[:], gate_w).then_inc(row_in, 16)
            sp.dma_start(w_in[0], Wq).then_inc(wl_in[0], 16)
            sp.dma_start(mask[:], c_mask).then_inc(c_in, 16)
            sp.dma_start(bo_all[:], bo.rearrange("(a n) -> a n", a=1).broadcast_to([P, D])).then_inc(c_in, 16)
            for k in range(1, NS):
                sp.dma_start(x_sb[:, k * SC:(k + 1) * SC, :], xv[:, k * SC:(k + 1) * SC, :]).then_inc(x_in[k], 16)
            sp.dma_start(b2_sb[:], b2).then_inc(c_in, 16)
            sp.dma_start(iota[:], c_iota).then_inc(c_in, 16)
            sp.dma_start(wo_sb[:], Wo.rearrange("(b p) n -> p b n", p=P)).then_inc(c_in, 16)
            for j in range(EJ):
                sp.dma_start(w1_in[:, j, :], w1[j]).then_inc(w1_load[j], 16)
                sp.dma_start(w2_in[:, j, :, :], w2[j].rearrange("(b p) d -> p b d", p=P)).then_inc(w2_load[j], 16)
            with sp.Fori(0, NS) as i:
                sp.wait_ge(cT_ok, i + 1)
                sp.dma_start(rows[:, bass.ds(i * ST, ST)], combT[:].rearrange("e c p -> e (c p)")
                             ).then_inc(comb_out, 16)
            sp.wait_ge(comb_out, 16 * NS)
            for j in range(EJ):
                sp.dma_start(comb_row[:, j, (NS - 1) * ST:], rows[j:j + 1, (NS - 1) * ST:].broadcast_to([P, ST])
                             ).then_inc(comb_load[j], 16)
            with sp.Fori(1, E // EJ) as i:
                for j in range(EJ):
                    sp.wait_ge(w1hi_ok, i * EJ + (j + 1 - EJ))
                    sp.wait_ge(w1lo_ok, i * EJ + (j + 1 - EJ))
                    sp.dma_start(w1_in[:, j, :], w1[bass.ds(i * EJ + j, 1), :, :].rearrange("e d f -> d (e f)")
                                 ).then_inc(w1_load[j], 16)
                    sp.wait_ge(w2hi_ok, i * EJ + (j + 1 - EJ))
                    sp.wait_ge(w2lo_ok, i * EJ + (j + 1 - EJ))
                    sp.dma_start(w2_in[:, j, :, :], w2[bass.ds(i * EJ + j, 1), :, :].rearrange("e (b p) d -> p (e b) d", p=P)
                                 ).then_inc(w2_load[j], 16)
                for j in range(EJ):
                    sp.wait_ge(part_ok, i * STEPS + (j + 1 - EJ) * NS)
                    sp.dma_start(comb_row[:, j, :], rows[bass.ds(i * EJ + j, 1), :].broadcast_to([P, T])
                                 ).then_inc(comb_load[j], 16)
            ov = out.rearrange("a (c p) d -> p (a c) d", p=P)
            for k in range(NS):
                sp.wait_ge(out_ok, k + 1)
                sp.dma_start(ov[:, k * SC:(k + 1) * SC, :], acc[:, k * SC:(k + 1) * SC, :]).then_inc(stored, 16)
            sp.wait_ge(stored, 16 * NS)

        @block.gpsimd
        def _(pool):
            pool.memset(neg_half[:], -0.5).then_inc(memsets, 1)
            pool.memset(state[:], 0.0).then_inc(memsets, 1)
            pool.memset(x_sb[:, NC:, :], 0.0).then_inc(memsets, 1)
            pool.memset(mv[:, NC:, :], 0.0).then_inc(memsets, 1)
            pool.memset(rstd[:, NC:], 0.0).then_inc(memsets, 1)
            pool.wait_ge(memsets, 5)
            for k in range(NS):
                pool.wait_ge(var1, k + 1)
                pool.tensor_tensor(rstd[:, k * SC:(k + 1) * SC], veps[:, k * SC:(k + 1) * SC],
                                   neg_half[:, 0:SC], ALU.pow).then_inc(rstd1_ok, 1)

            def normalise(i, c):
                pool.wait_ge(rden_ok, i * SC + c + 1)
                if c >= 2:
                    pool.wait_ge(oT_ps, i * 2 * SC + 2 * (c - 1))
                pool.tensor_tensor(on[:, c % 2, :, :], tcs[:, c % 2, :, 0:DH],
                                   rden[:, c % 2, :, None].broadcast_to([P, H, DH]), ALU.mult
                                   ).then_inc(on_ok, 1)

            def tail(i):
                pool.wait_ge(var2, i + 1)
                pool.tensor_tensor(rstd2[:], veps2[:], neg_half[:, 0:SC], ALU.pow).then_inc(rstd2_ok, 1)
                pool.wait_ge(yThi_ok, i + 1)
                pool.tensor_copy(yTall[:, 0, bass.ds(i * ST, ST)], f32(yT_hi[:])).then_inc(yT_all, 1)
                pool.wait_ge(yTlo_ok, i + 1)
                pool.tensor_copy(yTall[:, 1, bass.ds(i * ST, ST)], f32(yT_lo[:])).then_inc(yT_all, 1)

            for c in range(SC):
                normalise(0, c)
            with pool.Fori(1, NS) as i:
                tail(i - 1)
                for c in range(SC):
                    if c < 2:
                        pool.wait_ge(oT_ps, (i - 1) * 2 * SC + 2 * (c + SC - 1))
                    normalise(i, c)
            pool.wait_ge(o_ps, NS * GROUPS)
            pool.memset(accT[:], 0.0).then_inc(accT_zero, 1)
            pool.wait_ge(comb_out, 16 * (NS - 1))
            pool.wait_ge(v_rot, NS * V_JOBS)
            for j in range(EJ):
                pool.dma_start(comb_row[:, j, 0:(NS - 1) * ST], rows[j:j + 1, 0:(NS - 1) * ST]
                               .broadcast_to([P, (NS - 1) * ST])).then_inc(comb_early, 16)
            tail(NS - 1)

            def add(i, n):
                s = step(n)[1]
                pool.wait_ge(part_ok, i * STEPS + n + 1)
                pool.tensor_tensor(accT[:, s * ST:(s + 1) * ST], accT[:, s * ST:(s + 1) * ST],
                                   part[:, n % 2, :], ALU.add).then_inc(accT_ok, 1)

            pool.wait_ge(accT_zero, 1)
            for n in range(AHEAD - 1):
                add(0, n)
            with pool.Fori(0, E // EJ - 1) as i:
                for m in range(STEPS):
                    add(i, m + AHEAD - 1)
            for n in range(AHEAD - 1, NS):
                add(E // EJ - 1, n)

        @block.scalar
        def _(act):
            act.dma_start(brows[0:NP, :], bq.rearrange("(r p) -> r p", p=P)).then_inc(brow_in, 16)
            act.dma_start(brows[NP:2 * NP, :], bk.rearrange("(r p) -> r p", p=P)).then_inc(brow_in, 16)
            act.dma_start(brows[2 * NP:, :], b1.rearrange("e (b p) -> (e b) p", p=P)).then_inc(brow_in, 16)
            act.wait_ge(memsets, 1)
            act.activation(warm[:], neg_half[:, 0:1], ACT.Gelu)
            for k in (1, 2, 0):
                act.wait_ge(wl_in[k], 16)
                act.activation(w_hi[k][:], w_in[k], ACT.Copy).then_inc(whi_ok, 1)
                if k == 1:
                    act.wait_ge(bT_ps, 1)
                    act.activation(bcols[:], ps[:, 7, 0:2 * NP + E * FB], ACT.Copy).then_inc(bT_ok, 1)
                    act.wait_ge(xT_ps, 1)
                    act.activation(xT_hi[:], ps[:, 6, :], ACT.Copy).then_inc(xThi_ok, 1)
            act.wait_ge(row_in, 16 * 4)
            act.activation(gate_hi[:], gate_sb[:], ACT.Copy).then_inc(whi_ok, 1)
            act.wait_ge(bT_ok, 1)

            def turn_out(i, c):
                for half in range(2):
                    act.wait_ge(oT_ps, i * 2 * SC + 2 * c + half + 1)
                    act.activation(oT[:, c % 2, half * 4:half * 4 + 4, :],
                                   ps[:, 6 + half, :].rearrange("p (a b) -> p a b", b=P), ACT.Copy
                                   ).then_inc(oT_ok, 1)

            def front(i, tail):
                def rectified(t):
                    m = TOK[t][1]
                    act.wait_ge(tok_ok, i * TOK_JOBS + t + 1)
                    half = kn[:, m // 2, (m % 2) * 512:(m % 2) * 512 + 512]
                    act.activation(half, half, ACT.Relu).then_inc(kn_ok, 1)

                for j in range(QK_JOBS):
                    dst = (kT if j < NP else qT)[:, j % NP, :]
                    col = (NP if j < NP else 0) + j % NP
                    act.wait_ge(big_ps, i * QK_JOBS + j + 1)
                    act.activation(dst, ps[:, j % 4, :], ACT.Relu, bias=bcols[:, col:col + 1]).then_inc(big_ok, 1)
                    if j >= 2 and TOK[j - 2][0] == "k":
                        rectified(j - 2)
                    if tail and j == OT_AT:
                        turn_out(i - 1, SC - 1)
                    if tail and j == YT_AT:
                        act.wait_ge(yT_ps, i)
                        act.activation(yT_hi[:], ps[:, 6, :], ACT.Copy).then_inc(yThi_ok, 1)

            def x_turned(i):
                act.wait_ge(xT_ps, i + 1)
                act.activation(xT_hi[:], ps[:, 6, :], ACT.Copy).then_inc(xThi_ok, 1)

            def comb_turned(i):
                act.wait_ge(cT_ps, i + 1)
                act.activation(combT[:], ps[0:E, 7, :].rearrange("p (a b) -> p a b", b=P), ACT.Copy).then_inc(cT_ok, 1)

            def cos_part(i, n):
                c = n // NG
                act.wait_ge(o_ps, i * GROUPS + n + 1)
                if n >= 2:
                    act.wait_ge(tcs_ok, i * GROUPS + n - 1)
                act.activation(tc[:, n % 2, :, :, :],
                               ps[:, 2 + 2 * (n % 2):4 + 2 * (n % 2), 0:2 * CS]
                               .rearrange("p a (b s v) -> p a b s v", b=2, s=2)[:, :, :, 0, :],
                               ACT.Copy, scale=cs4[:, 0, c:c + 1]).then_inc(tc_ok, 1)

            def attention(i, tail):
                for n in range(GROUPS - 1):
                    c, g = n // NG, n % NG
                    if g == 2 and c >= 1:
                        turn_out(i, c - 1)
                    cos_part(i, n)
                    if tail and n == 1:
                        act.wait_ge(gap_ok, i)
                        act.activation(th[:], gap[:], ACT.Tanh, scale=0.5).then_inc(th_ok, 1)
                    if tail and n == 3:
                        comb_turned(i - 1)
                    if n == GROUPS - 2:
                        x_turned(i + 1)
                if tail:
                    act.wait_ge(comb_out, i * 16)

            front(0, False)
            attention(0, False)
            with act.Fori(1, NS) as i:
                cos_part(i - 1, GROUPS - 1)
                front(i, True)
                attention(i, True)

            def w1_high(i, j):
                act.wait_ge(w1_load[j], i * 16 + 16)
                act.activation(b1_now[:, j * FB:(j + 1) * FB],
                               bcols[:, bass.ds((i * EJ + j) * FB + 2 * NP, FB)], ACT.Copy).then_inc(b1_ok, 1)
                act.activation(w1_hi[:, j, :], w1_in[:, j, :], ACT.Copy).then_inc(w1hi_ok, 1)

            def w2_high(i, j):
                act.wait_ge(w2_load[j], i * 16 + 16)
                act.activation(w2_hi[:, j, :, :], w2_in[:, j, :, :], ACT.Copy).then_inc(w2hi_ok, 1)

            def hidden(i, n):
                j = step(n)[0]
                if n % NS == 0:
                    act.wait_ge(b1_ok, i * EJ + n // NS + 1)
                for b in range(FB):
                    act.wait_ge(h_ps, (i * STEPS + n) * FB + b + 1)
                    if n > 0:
                        act.wait_ge(hlo_ok, (i * STEPS + n - 1) * FB + b + 1)
                    act.activation(hT[:, b, :], ps[:, b, :], ACT.Gelu,
                                   bias=b1_now[:, j * FB + b:j * FB + b + 1]).then_inc(h_ok, 1)

            w1_high(0, 0)
            cos_part(NS - 1, GROUPS - 1)
            act.wait_ge(o_ps, NS * GROUPS)
            w2_high(0, 0)
            hidden(0, 0)
            turn_out(NS - 1, SC - 1)
            w1_high(0, 1)
            hidden(0, 1)
            hidden(0, 2)
            act.wait_ge(yT_ps, NS)
            act.activation(yT_hi[:], ps[:, 6, :], ACT.Copy).then_inc(yThi_ok, 1)
            w2_high(0, 1)
            act.wait_ge(gap_ok, NS)
            act.activation(th[:], gap[:], ACT.Tanh, scale=0.5).then_inc(th_ok, 1)
            hidden(0, 3)
            comb_turned(NS - 1)
            with act.Fori(0, E // EJ - 1) as i:
                for m in range(STEPS):
                    hidden(i, m + AHEAD)
                    if m % NS == 1:
                        w1_high(i + 1, m // NS)
                    if m % NS == 2:
                        act.wait_ge(y_ps, i * STEPS + (m // NS + 1) * NS)
                        w2_high(i + 1, m // NS)
            for n in range(AHEAD, STEPS):
                hidden(E // EJ - 1, n)

        @block.vector
        def _(dve):
            def norm1_stats(k):
                dve.wait_ge(x_in[k], 16)
                for c in range(k * SC, (k + 1) * SC):
                    last = dve.bn_stats(st6[:, c, :], x_sb[:, c, :])
                last.then_inc(bn1_ok, 1)
                dve.wait_ge(bn1_ok, k + 1)
                for c in range(k * SC, (k + 1) * SC):
                    last = dve.bn_aggr(mv[:, c, :], st6[:, c, :])
                last.then_inc(mv1_ok, 1)
                dve.wait_ge(mv1_ok, k + 1)
                dve.tensor_scalar(veps[:, k * SC:(k + 1) * SC], mv[:, k * SC:(k + 1) * SC, 1], EPS, None, ALU.add
                                  ).then_inc(var1, 1)

            def normed(i):
                for c in range(SC):
                    dve.tensor_scalar(xh[:, c, :], x_sb[:, bass.ds(i * SC + c, 1), :].rearrange("p a d -> p (a d)"),
                                      mv[:, bass.ds(i * SC + c, 1), 0], rstd[:, bass.ds(i * SC + c, 1)],
                                      ALU.subtract, ALU.mult).then_inc(xh_ok, 1)

            def low_half(k, count):
                dve.wait_ge(whi_ok, count)
                dve.tensor_tensor(w_lo[k][:], w_in[k], f32(w_hi[k][:]), ALU.subtract).then_inc(wlo_ok, 1)

            def angles(i):
                dve.tensor_copy(cs4[:], rot[:, :, bass.ds(i * SC, SC)]).then_inc(cs_ok, 1)

            def x_low(i):
                dve.wait_ge(xThi_ok, i + 1)
                dve.tensor_tensor(xT_lo[:], ps[:, 6, :], f32(xT_hi[:]), ALU.subtract).then_inc(xTlo_ok, 1)

            def ones_columns(i):
                dve.wait_ge(cs_ok, i + 1)
                for c in range(SC):
                    for s in range(2):
                        last = dve.tensor_copy(vcs[:, c, :, s, DH], cs4[:, s, c:c + 1].broadcast_to([P, H]))
                last.then_inc(vone, 1)

            def values(i, m):
                t = TOK.index(("v", m))
                dve.wait_ge(tok_ps, i * TOK_JOBS + t + 1)
                if m >= 2:
                    dve.wait_ge(v_rot, i * V_JOBS + m - 1)
                dve.tensor_tensor(vb[:, m % 2, :], ps[:, 4 + t % 2, :], bv_all[:, (m % 2) * 512:(m % 2) * 512 + 512],
                                  ALU.add).then_inc(tok_ok, 1)
                dve.wait_ge(tok_ok, i * TOK_JOBS + t + 1)
                for s in range(2):
                    last = dve.tensor_scalar(vcs[:, m // 2, (m % 2) * 8:(m % 2) * 8 + 8, s, 0:DH],
                                             vb[:, m % 2, :].rearrange("p (h d) -> p h d", d=DH),
                                             cs4[:, s, m // 2:m // 2 + 1], None, ALU.mult)
                last.then_inc(v_rot, 1)

            def keys(i, m):
                t = TOK.index(("k", m))
                dve.wait_ge(tok_ps, i * TOK_JOBS + t + 1)
                dve.tensor_tensor(kn[:, m // 2, (m % 2) * 512:(m % 2) * 512 + 512], ps[:, 4 + t % 2, :],
                                  bk_all[:, (m % 2) * 512:(m % 2) * 512 + 512], ALU.add).then_inc(tok_ok, 1)

            def front(i, tail):
                angles(i)
                ones_columns(i)
                for t, (kind, m) in enumerate(TOK):
                    if t == TOK_JOBS - 2:
                        if not tail:
                            dve.wait_ge(c_in, 16 * 5)
                        masked(i, 0)
                    (keys if kind == "k" else values)(i, m)
                    if not tail and t == 1:
                        low_half(0, 3)
                        dve.wait_ge(whi_ok, 4)
                        dve.tensor_tensor(gate_lo[:], gate_sb[:], f32(gate_hi[:]), ALU.subtract).then_inc(wlo_ok, 1)
                    if tail and t == STATS_AFTER:
                        norm2_stats(i - 1)
                    if tail and t == NORM_AFTER:
                        norm2(i - 1)
                    if tail and t in NORMED_AFTER:
                        normed2(i - 1, NORMED_AFTER.index(t))
                    if tail and t == YLOW_AFTER:
                        y_low(i - 1)

            def masked(i, n):
                dve.wait_ge(sc_ps, i * GROUPS + n + 1)
                if n >= 2:
                    dve.wait_ge(o_ps, i * GROUPS + n - 1)
                dve.tensor_tensor(am[:, n % 2, :, :].rearrange("p r (q t) -> p r q t", t=P),
                                  ps[:, 0:2, 0:2 * P].rearrange("p r (q t) -> p r q t", t=P),
                                  mask[:, None, None, :].broadcast_to([P, 2, 2, P]), ALU.mult).then_inc(am_ok, 1)

            def taken(i, n):
                c, g = n // NG, n % NG
                ob = ps[:, 2 + 2 * (n % 2):4 + 2 * (n % 2), :]
                if g == 0 and c >= 2:
                    dve.wait_ge(on_ok, i * SC + c - 1)
                dve.wait_ge(tc_ok, i * GROUPS + n + 1)
                dve.tensor_tensor(state[:, 2 * g:2 * g + 2, :], ob[:, :, 2 * CS:3 * CS],
                                  state[:, 2 * g:2 * g + 2, :], ALU.add).then_inc(st_ok, 1)
                for r in range(2):
                    last = dve.scalar_tensor_tensor(
                        out=tcs[:, c % 2, g * GH + r:(g + 1) * GH:2, :],
                        in0=ob[:, r, 0:2 * CS].rearrange("p (b s v) -> p b s v", b=2, s=2)[:, :, 1, :],
                        scalar=cs4[:, 1, c:c + 1], in1=tc[:, n % 2, r, :, :],
                        op0=ALU.mult, op1=ALU.add)
                last.then_inc(tcs_ok, 1)
                if g == NG - 1:
                    dve.wait_ge(tcs_ok, i * GROUPS + n + 1)
                    dve.tensor_scalar(dmax[:, c % 2, :], tcs[:, c % 2, :, DH], DEN_MIN, None, ALU.max
                                      ).then_inc(dmax_ok, 1)
                    dve.wait_ge(dmax_ok, i * SC + c + 1)
                    dve.reciprocal(rden[:, c % 2, :], dmax[:, c % 2, :]).then_inc(rden_ok, 1)

            def residual(i, c):
                dve.wait_ge(wo_ps, i * SC + c + 1)
                dve.tensor_tensor(x2[:, c, :], ps[:, 7, 0:D], x2[:, c, :], ALU.add).then_inc(x2_ok, 1)

            def norm2_stats(i):
                residual(i, SC - 1)
                dve.wait_ge(x2_ok, i * SC + SC)
                dve.memset(holder[:], 0.0)
                for c in range(SC):
                    last = dve.bn_stats(st62[:, c, :], x2[:, c, :])
                last.then_inc(bn2_ok, 1)

            def norm2(i):
                dve.wait_ge(bn2_ok, i + 1)
                dve.memset(holder[:], 0.0)
                for c in range(SC):
                    last = dve.bn_aggr(mv2[:, c, :], st62[:, c, :])
                last.then_inc(mv2_ok, 1)
                dve.wait_ge(mv2_ok, i + 1)
                dve.tensor_scalar(veps2[:], mv2[:, :, 1], EPS, None, ALU.add).then_inc(var2, 1)

            def normed2(i, half):
                dve.wait_ge(rstd2_ok, i + 1)
                for c in range(half * SC // 2, (half + 1) * SC // 2):
                    last = dve.tensor_scalar(yh[:, c, :], x2[:, c, :], mv2[:, c, 0:1], rstd2[:, c:c + 1],
                                             ALU.subtract, ALU.mult)
                last.then_inc(yh_ok, 1)

            def y_low(i):
                dve.wait_ge(yThi_ok, i + 1)
                dve.tensor_tensor(yT_lo[:], ps[:, 6, :], f32(yT_hi[:]), ALU.subtract).then_inc(yTlo_ok, 1)

            def best_two(i):
                dve.wait_ge(lg_ps, i + 1)
                dve.tensor_copy(lg[:], ps[:, 7, 0:SC * E].rearrange("p (c e) -> p c e", e=E)).then_inc(lg_ok, 1)
                dve.wait_ge(lg_ok, i + 1)
                dve.memset(holder[:], 0.0)
                for c in range(SC):
                    last = dve.max(top[:, c, :], lg[:, c, :])
                last.then_inc(top_ok, 1)
                dve.wait_ge(top_ok, i + 1)
                dve.tensor_tensor(gap[:], top[:, :, 0], top[:, :, 1], ALU.subtract).then_inc(gap_ok, 1)
                for c in range(SC):
                    last = dve.max_index(idx[:, c, :], top[:, c, :], lg[:, c, :])
                last.then_inc(idx_ok, 1)
                dve.wait_ge(idx_ok, i + 1)
                dve.tensor_copy(idxf[:], idx[:, :, 0:2]).then_inc(idxf_ok, 1)

            def combine(i):
                dve.wait_ge(idxf_ok, i + 1)
                dve.wait_ge(th_ok, i + 1)
                dve.tensor_scalar(wts[:, 0, :], th[:], 0.5, 0.5, ALU.mult, ALU.add)
                dve.tensor_scalar(wts[:, 1, :], th[:], -0.5, 0.5, ALU.mult, ALU.add).then_inc(wts_ok, 1)
                each = [P, 2, SC, E]
                dve.tensor_tensor(hot[:], iota[:, None, None, :].broadcast_to(each),
                                  idxf[:].rearrange("p c k -> p k c")[:, :, :, None].broadcast_to(each),
                                  ALU.is_equal).then_inc(hot_ok, 1)
                dve.wait_ge(wts_ok, i + 1)
                dve.wait_ge(hot_ok, i + 1)
                dve.tensor_tensor(hot[:], hot[:], wts[:, :, :, None].broadcast_to(each), ALU.mult).then_inc(hotw_ok, 1)
                dve.wait_ge(hotw_ok, i + 1)
                dve.tensor_tensor(comb[:], hot[:, 0, :, :], hot[:, 1, :, :], ALU.add).then_inc(comb_ok, 1)

            def open_sum(i):
                dve.wait_ge(b2_ps, i + 1)
                dve.tensor_tensor(acc[:, bass.ds(i * SC, SC), :], ps[:, 6, :].rearrange("p (c d) -> p c d", d=D),
                                  x2[:], ALU.add).then_inc(acc0_ok, 1)

            def open_residual(i):
                dve.tensor_tensor(x2[:], x_sb[:, bass.ds(i * SC, SC), :],
                                  bo_all[:, None, :].broadcast_to([P, SC, D]), ALU.add).then_inc(x2_open, 1)

            def finish(i):
                taken(i, GROUPS - 1)
                residual(i, SC - 2)

            def attention(i, tail):
                for n in range(GROUPS):
                    if tail and n == 6:
                        open_sum(i - 1)
                        dve.wait_ge(acc0_ok, i)
                    if n >= 1:
                        masked(i, n)
                        taken(i, n - 1)
                    if tail and n == 1:
                        best_two(i - 1)
                    if tail and n == 3:
                        combine(i - 1)
                    if not tail and 1 <= n < NS:
                        norm1_stats(n)
                    if n == 7:
                        open_residual(i)
                    if n == 2 * NG:
                        if not tail:
                            dve.wait_ge(rstd1_ok, NS)
                        normed(i + 1)
                    if n % NG == 1 and n > 2 * NG:
                        if n // NG == 2:
                            dve.wait_ge(x2_open, i + 1)
                        residual(i, n // NG - 2)
                x_low(i + 1)

            norm1_stats(0)
            dve.wait_ge(rstd1_ok, 1)
            normed(0)
            low_half(1, 1)
            x_low(0)
            low_half(2, 2)
            dve.wait_ge(row_in, 16 * 4)
            front(0, False)
            dve.wait_ge(memsets, 5)
            attention(0, False)
            with dve.Fori(1, NS) as i:
                finish(i - 1)
                front(i, True)
                attention(i, True)

            def w1_low(i, j):
                dve.wait_ge(w1hi_ok, i * EJ + j + 1)
                dve.tensor_tensor(w1_lo[:, j, :], w1_in[:, j, :], f32(w1_hi[:, j, :]), ALU.subtract
                                  ).then_inc(w1lo_ok, 1)

            def w2_low(i, j):
                dve.wait_ge(w2hi_ok, i * EJ + j + 1)
                dve.tensor_tensor(w2_lo[:, j, :, :], w2_in[:, j, :, :], f32(w2_hi[:, j, :, :]), ALU.subtract
                                  ).then_inc(w2lo_ok, 1)

            def halves(i, n):
                if n >= 2:
                    dve.wait_ge(y_ps, i * STEPS + n - 1)

                def low(b):
                    dve.wait_ge(hhi_ok, (i * STEPS + n) * FB + b + 1)
                    dve.tensor_tensor(hT_lo[:, n % 2, b, :], hT[:, b, :], f32(hT_hi[:, n % 2, b, :]), ALU.subtract
                                      ).then_inc(hlo_ok, 1)
                for b in range(FB):
                    dve.wait_ge(h_ok, (i * STEPS + n) * FB + b + 1)
                    dve.tensor_copy(hT_hi[:, n % 2, b, :], hT[:, b, :]).then_inc(hhi_ok, 1)
                    if b:
                        low(b - 1)
                low(FB - 1)

            def weigh(i, n, early=False, last=False):
                j, s = step(n)
                dve.wait_ge(y_ps, i * STEPS + n + 1)
                if n >= 2 and not last:
                    dve.wait_ge(accT_ok, i * STEPS + n - 1)
                if last and s >= 2:
                    dve.wait_ge(accT_end, s - 1)
                if not early and s in (0, NS - 1):
                    dve.wait_ge(comb_load[j], (i + n // STEPS) * 16 + 16)
                dve.tensor_tensor(part[:, n % 2, :], ps[:, 4 + n % 2, :], comb_row[:, j, s * ST:(s + 1) * ST],
                                  ALU.mult).then_inc(part_ok, 1)

            def add_last(k):
                dve.wait_ge(accT_ok, E * NS - NS)
                dve.wait_ge(part_ok, E * NS - NS + k + 1)
                dve.tensor_tensor(accT[:, k * ST:(k + 1) * ST], accT[:, k * ST:(k + 1) * ST],
                                  part[:, k % 2, :], ALU.add).then_inc(accT_end, 1)

            def store(k):
                dve.wait_ge(back_ps, k + 1)
                dve.tensor_tensor(acc[:, k * SC:(k + 1) * SC, :], ps[:, 6 + k % 2, :].rearrange("p (c d) -> p c d", d=D),
                                  acc[:, k * SC:(k + 1) * SC, :], ALU.add).then_inc(out_ok, 1)

            w1_low(0, 0)
            finish(NS - 1)
            dve.wait_ge(o_ps, NS * GROUPS)
            w2_low(0, 0)
            halves(0, 0)
            w1_low(0, 1)
            halves(0, 1)
            norm2_stats(NS - 1)
            norm2(NS - 1)
            normed2(NS - 1, 0)
            normed2(NS - 1, 1)
            dve.wait_ge(comb_early, 16 * EJ)
            weigh(0, 0, early=True)
            halves(0, 2)
            y_low(NS - 1)
            w2_low(0, 1)
            weigh(0, 1, early=True)
            best_two(NS - 1)
            combine(NS - 1)
            weigh(0, 2, early=True)
            halves(0, 3)
            open_sum(NS - 1)
            with dve.Fori(0, E // EJ - 1) as i:
                for m in range(STEPS):
                    halves(i, m + AHEAD)
                    weigh(i, m + AHEAD - 1)
                    if m % NS == 1:
                        w1_low(i + 1, m // NS)
                    if m % NS == 2:
                        w2_low(i + 1, m // NS)
            for n in range(AHEAD - 1, STEPS):
                if n + 1 < STEPS:
                    halves(E // EJ - 1, n + 1)
                if n > NS:
                    add_last(n - NS - 1)
                weigh(E // EJ - 1, n, last=n >= NS + 2)
                if n > NS + 1:
                    store(n - NS - 2)
            add_last(NS - 1)
            store(NS - 2)
            store(NS - 1)

        @block.tensor
        def _(pe):
            mm = pe.matmul
            def split3(o, a, b, part_a, part_b):
                mm(o, part_a(a[0]), part_b(b[0]), start=True, stop=False)
                mm(o, part_a(a[0]), part_b(b[1]), start=False, stop=False)
                return mm(o, part_a(a[1]), part_b(b[0]), start=False, stop=True)

            def turn_x(i):
                for c in range(SC):
                    pe.wait_ge(xh_ok, i * SC + c + 1)
                    last = pe.transpose(ps[:, 6, c * P:(c + 1) * P], xh[:, c, :], ident[:])
                last.then_inc(xT_ps, 1)

            def front(i, tail):
                pe.wait_ge(xThi_ok, i + 1)
                pe.wait_ge(xTlo_ok, i + 1)

                def block(j):
                    if j >= 4:
                        pe.wait_ge(big_ok, i * QK_JOBS + j - 3)
                    if not tail and j == NP:
                        pe.wait_ge(whi_ok, 3)
                        pe.wait_ge(wlo_ok, 3)
                    w, b = 1 if j < NP else 0, j % NP
                    split3(ps[:, j % 4, :], (w_hi[w], w_lo[w]), (xT_hi, xT_lo),
                           lambda t: t[:, b * P:(b + 1) * P], lambda t: t[:]).then_inc(big_ps, 1)

                def tokens(t):
                    kind, m = TOK[t]
                    if t >= 2:
                        pe.wait_ge(tok_ok, i * TOK_JOBS + t - 1)
                    if not tail and (kind, m) == ("v", 0):
                        pe.wait_ge(whi_ok, 2)
                        pe.wait_ge(wlo_ok, 2)
                    w, c, half = (1 if kind == "k" else 2), m // 2, m % 2
                    split3(ps[:, 4 + t % 2, :], (xT_hi, xT_lo), (w_hi[w], w_lo[w]),
                           lambda t: t[:, c * P:(c + 1) * P], lambda t: t[:, half * 512:half * 512 + 512]
                           ).then_inc(tok_ps, 1)

                for j in range(QK_JOBS):
                    if tail and j == 2:
                        pe.wait_ge(tcs_ok, i * GROUPS)
                    block(j)
                    if j == QK_JOBS - 1:
                        scores(i, 0)
                    if j >= 2:
                        tokens(j - 2)
                    if tail and j == OT_AT:
                        turn_out(i - 1, SC - 1)
                    if tail and j == WO_AT:
                        project(i - 1, SC - 1)
                    if tail and j == YT_AT:
                        turn_y(i - 1)
                    if tail and j == GATE_AT:
                        gate(i - 1)
                tokens(TOK_JOBS - 2)
                tokens(TOK_JOBS - 1)

            def scores(i, n):
                if n == 0:
                    pe.wait_ge(big_ok, i * QK_JOBS + QK_JOBS - 2)
                c, g = n // NG, n % NG
                if n >= 1:
                    pe.wait_ge(am_ok, i * GROUPS + n)
                for h in range(g * GH, (g + 1) * GH):
                    r = slice(64 * (h % 2), 64 * (h % 2) + 64)
                    col = (h % GH) // 2 * P
                    last = mm(ps[:, h % 2, col:col + P], kT[r, h // 2, c * P:(c + 1) * P],
                              qT[r, h // 2, c * P:(c + 1) * P], start=True, stop=True)
                last.then_inc(sc_ps, 1)

            def outputs(i, n):
                c, g = n // NG, n % NG
                pe.wait_ge(am_ok, i * GROUPS + n + 1)
                if n == 0:
                    pe.wait_ge(big_ok, i * QK_JOBS + QK_JOBS)
                if n == 1:
                    pe.wait_ge(tok_ok, i * TOK_JOBS + TOK_JOBS)
                if n >= 2:
                    pe.wait_ge(tcs_ok, i * GROUPS + n - 1)
                    pe.wait_ge(st_ok, i * GROUPS + n - 1)
                if c >= 1:
                    pe.wait_ge(st_ok, i * GROUPS + n - NG + 1)
                if g == 0:
                    pe.wait_ge(v_rot, i * V_JOBS + 2 * c + 2)
                    pe.wait_ge(kn_ok, i * K_JOBS + 2 * c + 2)
                    pe.wait_ge(vone, i + 1)
                vh = lambda h: vcs[:, c, h, :, :].rearrange("p s v -> p (s v)")
                for h in range(g * GH, (g + 1) * GH):
                    q, r = h % GH // 2, h % 2
                    mm(ps[:, 2 + 2 * (n % 2) + r, q * CS:(q + 1) * CS], am[:, n % 2, r, q * P:(q + 1) * P],
                       vh(h), start=(q == 0), stop=False, skip_group_check=True)
                for h in range(g * GH, (g + 1) * GH):
                    q, r = h % GH // 2, h % 2
                    rows = slice(64 * r, 64 * r + 64)
                    mm(ps[:, 2 + 2 * (n % 2) + r, q * CS:(q + 1) * CS], qT[rows, h // 2, c * P:(c + 1) * P],
                       state[rows, h // 2, :], start=False, stop=True, skip_group_check=True)
                for h in range(g * GH, (g + 1) * GH):
                    q, r = h % GH // 2, h % 2
                    last = mm(ps[64 * r:64 * r + 64, 2 + 2 * (n % 2) + q, 2 * CS:3 * CS],
                              kn[:, c, h * DH:(h + 1) * DH], vh(h), start=True, stop=True, skip_group_check=True)
                last.then_inc(o_ps, 1)

            def turn_out(i, c):
                pe.wait_ge(on_ok, i * SC + c + 1)
                for half in range(2):
                    if half == 1 and c >= 1:
                        pe.wait_ge(x2_ok, i * SC + c)
                    for q in range(4):
                        pr = half * 4 + q
                        last = pe.transpose(ps[:, 6 + half, q * P:(q + 1) * P],
                                            on[:, c % 2, 2 * pr:2 * pr + 2, :].rearrange("p h d -> p (h d)"),
                                            ident[:])
                    last.then_inc(oT_ps, 1)

            def project(i, c):
                pe.wait_ge(oT_ok, i * 2 * SC + 2 * c + 2)
                for pr in range(NP):
                    last = mm(ps[:, 7, 0:D], oT[:, c % 2, pr, :], wo_sb[:, pr, :], start=(pr == 0), stop=(pr == NP - 1))
                last.then_inc(wo_ps, 1)

            def turn_y(i):
                pe.wait_ge(yh_ok, 2 * i + 2)
                for c in range(SC):
                    last = pe.transpose(ps[:, 6, c * P:(c + 1) * P], yh[:, c, :], ident[:])
                last.then_inc(yT_ps, 1)

            def gate(i):
                pe.wait_ge(yThi_ok, i + 1)
                pe.wait_ge(yTlo_ok, i + 1)
                for c in range(SC):
                    last = split3(ps[:, 7, c * E:(c + 1) * E], (yT_hi, yT_lo), (gate_hi, gate_lo),
                                  lambda t: t[:, c * P:(c + 1) * P], lambda t: t[:])
                last.then_inc(lg_ps, 1)

            def turn_comb(i):
                pe.wait_ge(comb_ok, i + 1)
                for c in range(SC):
                    last = pe.transpose(ps[0:E, 7, c * P:(c + 1) * P], comb[:, c, :], ident[:])
                last.then_inc(cT_ps, 1)

            def biases(i):
                pe.wait_ge(cT_ok, i + 1)
                for c in range(SC):
                    last = mm(ps[:, 6, c * D:(c + 1) * D], combT[:, c, :], b2_sb[:], start=True, stop=True)
                last.then_inc(b2_ps, 1)

            def attention(i, tail):
                for n in range(GROUPS + 1):
                    if 1 <= n < GROUPS:
                        scores(i, n)
                    if n >= 1:
                        outputs(i, n - 1)
                    if tail and n == 4:
                        turn_comb(i - 1)
                    if tail and n == 5:
                        biases(i - 1)
                    if n % NG == 2 and n >= NG:
                        if n // NG == 1 and tail:
                            pe.wait_ge(acc0_ok, i)
                        turn_out(i, n // NG - 1)
                    if n % NG == 0 and n >= 2 * NG:
                        project(i, n // NG - 2)
                    if n == GROUPS - 1:
                        pe.wait_ge(oT_ok, i * 2 * SC + 2 * (SC - 1))
                        turn_x(i + 1)

            pe.wait_ge(brow_in, 16 * 4)
            pe.transpose(ps[:, 7, 0:2 * NP + E * FB], brows[:], ident[0:2 * NP + E * FB, 0:2 * NP + E * FB]
                         ).then_inc(bT_ps, 1)
            turn_x(0)
            pe.wait_ge(bT_ok, 1)
            pe.wait_ge(whi_ok, 1)
            pe.wait_ge(wlo_ok, 1)
            front(0, False)
            attention(0, False)
            with pe.Fori(1, NS) as i:
                front(i, True)
                attention(i, True)

            def hidden(i, n, first=False):
                j, s = step(n)
                if s == 0:
                    pe.wait_ge(w1hi_ok, i * EJ + n // NS + 1)
                    pe.wait_ge(w1lo_ok, i * EJ + n // NS + 1)
                for b in range(FB):
                    if first and b == 2:
                        pe.wait_ge(tcs_ok, NS * GROUPS)
                        pe.wait_ge(st_ok, NS * GROUPS)
                    if n > 0:
                        pe.wait_ge(h_ok, (i * STEPS + n - 1) * FB + b + 1)
                    split3(ps[:, b, :], (w1_hi, w1_lo), (0, 1),
                           lambda t: t[:, j, b * P:(b + 1) * P], lambda t: yTall[:, t, s * ST:(s + 1) * ST]
                           ).then_inc(h_ps, 1)

            def down(i, n):
                j, s = step(n)
                if s == 0:
                    pe.wait_ge(w2hi_ok, i * EJ + n // NS + 1)
                    pe.wait_ge(w2lo_ok, i * EJ + n // NS + 1)
                if n >= 2:
                    pe.wait_ge(part_ok, i * STEPS + n - 1)
                o = ps[:, 4 + n % 2, :]
                for b in range(FB):
                    pe.wait_ge(hlo_ok, (i * STEPS + n) * FB + b + 1)
                    mm(o, w2_hi[:, j, b, :], hT_hi[:, n % 2, b, :], start=(b == 0), stop=False)
                    mm(o, w2_hi[:, j, b, :], hT_lo[:, n % 2, b, :], start=False, stop=False)
                    last = mm(o, w2_lo[:, j, b, :], hT_hi[:, n % 2, b, :], start=False, stop=(b == FB - 1))
                last.then_inc(y_ps, 1)

            def turn_back(k):
                if k >= 2:
                    pe.wait_ge(out_ok, k - 1)
                pe.wait_ge(accT_end, k + 1)
                for c in range(SC):
                    last = pe.transpose(ps[:, 6 + k % 2, c * D:(c + 1) * D],
                                        accT[:, k * ST + c * P:k * ST + (c + 1) * P], ident[:])
                last.then_inc(back_ps, 1)

            pe.wait_ge(am_ok, NS * GROUPS)
            pe.wait_ge(yT_all, 2 * (NS - 1))
            hidden(0, 0, first=True)
            pe.wait_ge(xThi_ok, NS + 1)
            pe.wait_ge(xTlo_ok, NS + 1)
            turn_out(NS - 1, SC - 1)
            hidden(0, 1)
            project(NS - 1, SC - 1)
            down(0, 0)
            hidden(0, 2)
            down(0, 1)
            turn_y(NS - 1)
            down(0, 2)
            gate(NS - 1)
            pe.wait_ge(yT_all, 2 * NS)
            hidden(0, 3)
            turn_comb(NS - 1)
            biases(NS - 1)
            with pe.Fori(0, E // EJ - 1) as i:
                for m in range(STEPS):
                    hidden(i, m + AHEAD)
                    down(i, m + AHEAD - 1)
            pe.wait_ge(acc0_ok, NS)
            for n in range(AHEAD - 1, STEPS):
                if n + 1 < STEPS:
                    hidden(E // EJ - 1, n + 1)
                down(E // EJ - 1, n)
                if n > NS + 1:
                    turn_back(n - NS - 2)
            turn_back(NS - 2)
            turn_back(NS - 1)


_INS = ["L0_attn_x", "L0_attn_Wq", "L0_attn_bq", "L0_attn_Wk", "L0_attn_bk", "L0_attn_Wv", "L0_attn_bv",
        "L0_attn_Wo", "L0_attn_bo", "L0_ffn_gate_w", "L0_ffn_w1", "L0_ffn_b1", "L0_ffn_w2", "L0_ffn_b2"]


def shape_constants():
    angles = np.float32(math.pi / (2.0 * T)) * np.arange(T, dtype=np.float32)
    rot = np.stack([np.cos(angles), np.sin(angles)]).astype(np.float32)
    rot = np.ascontiguousarray(rot.reshape(2, NC, P).transpose(2, 0, 1).reshape(P, 2 * NC))
    mask = np.triu(np.ones((P, P), np.float32))
    iota = np.tile(np.arange(E, dtype=np.float32), (P, 1))
    return {"c_rot": rot, "c_mask": mask, "c_ident": np.eye(P, dtype=np.float32), "c_iota": iota}


def kernel(**inputs):
    import concourse.bacc as bacc
    from concourse.bass_utils import run_bass_kernel_spmd

    nc = bacc.Bacc("TRN2", target_bir_lowering=False, num_devices=1)
    arrays = {f"in_{name}": np.ascontiguousarray(inputs[name]) for name in _INS}
    arrays.update(shape_constants())
    args = [nc.dram_tensor(n, a.shape, mybir.dt.from_np(a.dtype), kind="ExternalInput").ap()
            for n, a in arrays.items()]
    out = nc.dram_tensor("out", (1, T, D), F32, kind="ExternalOutput").ap()
    rows = nc.dram_tensor("rows", (E, T), F32).ap()
    moe_block(nc, *args, out, rows)
    r = run_bass_kernel_spmd(nc, [arrays], core_ids=[0])
    return r.results[0]["out"]
```

```python
import math
from contextlib import ExitStack

import numpy as np

import concourse.bass as bass
from concourse import mybir

ALU = mybir.AluOpType
ACT = mybir.ActivationFunctionType
F32 = mybir.dt.float32
F32R = mybir.dt.float32r
U32 = mybir.dt.uint32

P = 128
T, D = 2048, 128
H, DH = 16, 64
HD = H * DH
E, F = 8, 512
EPS = 1e-5
DEN_MIN = 1e-6
NC = T // P
SC = 4
NS = NC // SC
ST = SC * P
NP = H // 2
VW = DH + 1
CS = 2 * VW
GH = 4
NG = H // GH
FB = F // P
EJ = 2

QK_JOBS = 2 * NP
V_JOBS = 2 * SC
K_JOBS = 2 * SC
GROUPS = SC * NG

V_AT = {2 * _m + 2: _m for _m in range(V_JOBS - 1)}
K_AT = {NP + 1 + _m: _m for _m in range(K_JOBS - 1)}
OT_AT, WO_AT, YT_AT, GATE_AT = 3, 5, 11, 14
STATS_AFTER, NORM_AFTER, NORMED_AFTER, YLOW_AFTER, BEST_AFTER = 1, 2, 3, 5, 6

STEPS = EJ * NS
AHEAD = 4


def step(n):
    return n % STEPS // NS, n % NS


def moe_block(nc, x, Wq, bq, Wk, bk, Wv, bv, Wo, bo, gate_w, w1, b1, w2, b2,
              c_rot, c_pair, c_ident, c_iota, out, rows):
    with ExitStack() as ctx:
        def sb(name, shape, dt=F32):
            return ctx.enter_context(nc.sbuf_tensor(name, shape, dt))

        def sem(name):
            return ctx.enter_context(nc.semaphore(name))

        ps = ctx.enter_context(nc.psum_tensor("ps", [P, 8, 512], F32))

        x_sb = sb("x_sb", [P, NC + SC, D])
        w_hi = [sb(f"w_hi{k}", [P, HD], F32R) for k in range(3)]
        w_lo = [sb(f"w_lo{k}", [P, HD], F32R) for k in range(3)]
        wo_sb = sb("wo_sb", [P, NP, D])
        gate_sb = sb("gate_sb", [P, E])
        gate_hi = sb("gate_hi", [P, E], F32R)
        gate_lo = sb("gate_lo", [P, E], F32R)
        brows = sb("brows", [2 * NP + E * FB, P])
        bcols = sb("bcols", [P, 2 * NP + E * FB])
        bv_all = sb("bv_all", [P, HD])
        bo_all = sb("bo_all", [P, D])
        b2_sb = sb("b2_sb", [E, D])
        rot = sb("rot", [P, 2, NC])
        pair = sb("pair", [P, SC, P])
        ident = sb("ident", [P, P])
        iota = sb("iota", [P, E])
        neg_half = sb("neg_half", [P, NC])
        mv = sb("mv", [P, NC + SC, 2])
        st6 = sb("st6", [P, NC, 6])
        rstd = sb("rstd", [P, NC + SC])
        veps = sb("veps", [P, NC])
        xh = sb("xh", [P, SC, D])
        xT_hi = sb("xT_hi", [P, ST], F32R)
        xT_lo = sb("xT_lo", [P, ST], F32R)
        cs4 = sb("cs4", [P, 2, SC])
        am = sb("am", [P, 2, 2, 2 * P])
        state = sb("state", [P, NP, CS])
        tc = sb("tc", [P, 2, 2, GH // 2, VW])
        tcs = sb("tcs", [P, 2, H, VW])
        rden = sb("rden", [P, 2, H])
        dmax = sb("dmax", [P, 2, H])
        on = sb("on", [P, 2, H, DH])
        oT = sb("oT", [P, 2, NP, P])
        x2 = sb("x2", [P, SC, D])
        mv2 = sb("mv2", [P, SC, 2])
        st62 = sb("st62", [P, SC, 6])
        rstd2 = sb("rstd2", [P, SC])
        veps2 = sb("veps2", [P, SC])
        yh = xh
        yT_hi = sb("yT_hi", [P, ST], F32R)
        yT_lo = sb("yT_lo", [P, ST], F32R)
        yTall = sb("yTall", [P, 2, T], F32R)
        lg = sb("lg", [P, SC, E])
        top = sb("top", [P, SC, E])
        idx = sb("idx", [P, SC, E], U32)
        idxf = sb("idxf", [P, SC, 2])
        warm = sb("warm", [P, 1])
        holder = sb("holder", [P, 1])
        gap = sb("gap", [P, SC])
        th = sb("th", [P, SC])
        wts = sb("wts", [P, 2, SC])
        hot = sb("hot", [P, 2, SC, E])
        comb = sb("comb", [P, SC, E])
        combT = sb("combT", [E, SC, P])
        w1_in = sb("w1_in", [P, EJ, F])
        w1_hi = w_hi[0][:].rearrange("p (j f) -> p j f", j=EJ)
        w1_lo = w_lo[0][:].rearrange("p (j f) -> p j f", j=EJ)
        b1_now = sb("b1_now", [P, EJ * FB])
        w2_in = sb("w2_in", [P, EJ, FB, D])
        acc = x_sb
        attn = ExitStack()

        def sb_attn(name, shape):
            return attn.enter_context(nc.sbuf_tensor(name, shape, F32))

        qT = sb_attn("qT", [P, NP, ST])
        kT = sb_attn("kT", [P, NP, ST])
        kn = sb_attn("kn", [P, SC, HD])
        w_in = [kn[:, k, :] for k in (3, 1, 2)]
        vb = sb_attn("vb", [P, 2, HD // 2])
        vcs = sb_attn("vcs", [P, SC, H, 2, VW])
        attn.close()
        hT = sb("hT", [P, FB, ST])
        hT_hi = sb("hT_hi", [P, 2, FB, ST], F32R)
        hT_lo = sb("hT_lo", [P, 2, FB, ST], F32R)
        w2_hi = sb("w2_hi", [P, EJ, FB, D], F32R)
        w2_lo = sb("w2_lo", [P, EJ, FB, D], F32R)
        comb_row = sb("comb_row", [P, EJ, T])
        part = sb("part", [P, 2, ST])
        accT = sb("accT", [P, T])

        x_in = [sem(f"x_in{k}") for k in range(NS)]
        pair_in = [sem(f"pair_in{c}") for c in range(SC)]
        wl_in = [sem(f"wl_in{k}") for k in range(3)]
        w1_load = [sem(f"w1_load{j}") for j in range(EJ)]
        w2_load = [sem(f"w2_load{j}") for j in range(EJ)]
        comb_load = [sem(f"comb_load{j}") for j in range(EJ)]
        brow_in = sem("brow_in")
        row_in = sem("row_in")
        c_in = sem("c_in")
        comb_early = sem("comb_early")
        comb_out = sem("comb_out")
        stored = sem("stored")
        memsets = sem("memsets")
        bT_ps = sem("bT_ps")
        bT_ok = sem("bT_ok")
        whi_ok = sem("whi_ok")
        wlo_ok = sem("wlo_ok")
        bn1_ok = sem("bn1_ok")
        mv1_ok = sem("mv1_ok")
        var1 = sem("var1")
        rstd1_ok = sem("rstd1_ok")
        xh_ok = sem("xh_ok")
        xT_ps = sem("xT_ps")
        xThi_ok = sem("xThi_ok")
        xTlo_ok = sem("xTlo_ok")
        big_ps = sem("big_ps")
        big_ok = sem("big_ok")
        v_ps = sem("v_ps")
        v_add = sem("v_add")
        v_rot = sem("v_rot")
        kn_ps = sem("kn_ps")
        kn_ok = sem("kn_ok")
        cs_ok = sem("cs_ok")
        vone = sem("vone")
        sc_ps = sem("sc_ps")
        am_ok = sem("am_ok")
        o_ps = sem("o_ps")
        tc_ok = sem("tc_ok")
        tcs_ok = sem("tcs_ok")
        st_ok = sem("st_ok")
        dmax_ok = sem("dmax_ok")
        rden_ok = sem("rden_ok")
        on_ok = sem("on_ok")
        oT_ps = sem("oT_ps")
        oT_ok = sem("oT_ok")
        wo_ps = sem("wo_ps")
        x2_open = sem("x2_open")
        x2_ok = sem("x2_ok")
        bn2_ok = sem("bn2_ok")
        mv2_ok = sem("mv2_ok")
        var2 = sem("var2")
        rstd2_ok = sem("rstd2_ok")
        yh_ok = sem("yh_ok")
        yT_ps = sem("yT_ps")
        yThi_ok = sem("yThi_ok")
        yTlo_ok = sem("yTlo_ok")
        yT_all = sem("yT_all")
        lg_ps = sem("lg_ps")
        lg_ok = sem("lg_ok")
        top_ok = sem("top_ok")
        gap_ok = sem("gap_ok")
        th_ok = sem("th_ok")
        idx_ok = sem("idx_ok")
        idxf_ok = sem("idxf_ok")
        wts_ok = sem("wts_ok")
        hot_ok = sem("hot_ok")
        hotw_ok = sem("hotw_ok")
        comb_ok = sem("comb_ok")
        cT_ps = sem("cT_ps")
        cT_ok = sem("cT_ok")
        b2_ps = sem("b2_ps")
        acc0_ok = sem("acc0_ok")
        w1hi_ok = sem("w1hi_ok")
        w1lo_ok = sem("w1lo_ok")
        w2hi_ok = sem("w2hi_ok")
        w2lo_ok = sem("w2lo_ok")
        b1_ok = sem("b1_ok")
        h_ps = sem("h_ps")
        h_ok = sem("h_ok")
        heven_ok = sem("heven_ok")
        hodd_ok = sem("hodd_ok")
        hlo_ok = sem("hlo_ok")
        y_ps = sem("y_ps")
        part_ok = sem("part_ok")
        accT_zero = sem("accT_zero")
        accT_ok = sem("accT_ok")
        accT_end = sem("accT_end")
        back_ps = sem("back_ps")
        out_ok = sem("out_ok")

        block = ctx.enter_context(nc.Block())
        f32 = lambda ap: ap.bitcast(F32)

        @block.sync
        def _(sp):
            xv = x.rearrange("a (c p) d -> p (a c) d", p=P)
            sp.dma_start(x_sb[:, 0:SC, :], xv[:, 0:SC, :]).then_inc(x_in[0], 16)
            sp.dma_start(w_in[1], Wk).then_inc(wl_in[1], 16)
            sp.dma_start(ident[:], c_ident).then_inc(brow_in, 16)
            sp.dma_start(w_in[2], Wv).then_inc(wl_in[2], 16)
            sp.dma_start(rot[:], c_rot.rearrange("p (a c) -> p a c", a=2)).then_inc(row_in, 16)
            sp.dma_start(bv_all[:], bv.rearrange("(a n) -> a n", a=1).broadcast_to([P, HD])).then_inc(row_in, 16)
            sp.dma_start(gate_sb[:], gate_w).then_inc(row_in, 16)
            sp.dma_start(w_in[0], Wq).then_inc(wl_in[0], 16)
            for c in range(SC):
                sp.dma_start(pair[:, c, :], c_pair[:, c, :]).then_inc(pair_in[c], 16)
            sp.dma_start(bo_all[:], bo.rearrange("(a n) -> a n", a=1).broadcast_to([P, D])).then_inc(c_in, 16)
            for k in range(1, NS):
                sp.dma_start(x_sb[:, k * SC:(k + 1) * SC, :], xv[:, k * SC:(k + 1) * SC, :]).then_inc(x_in[k], 16)
            sp.dma_start(b2_sb[:], b2).then_inc(c_in, 16)
            sp.dma_start(iota[:], c_iota).then_inc(c_in, 16)
            sp.dma_start(wo_sb[:], Wo.rearrange("(b p) n -> p b n", p=P)).then_inc(c_in, 16)
            for j in range(EJ):
                sp.dma_start(w1_in[:, j, :], w1[j]).then_inc(w1_load[j], 16)
                sp.dma_start(w2_in[:, j, :, :], w2[j].rearrange("(b p) d -> p b d", p=P)).then_inc(w2_load[j], 16)
            with sp.Fori(1, NS) as i:
                for c in range(SC):
                    sp.wait_ge(am_ok, i * GROUPS - GROUPS + (c + 1) * NG)
                    sp.dma_start(pair[:, c, :], c_pair[:, bass.ds(i * SC + c, 1), :].rearrange("p a t -> p (a t)")
                                 ).then_inc(pair_in[c], 16)
                sp.wait_ge(cT_ok, i)
                sp.dma_start(rows[:, bass.ds(i * ST - ST, ST)], combT[:].rearrange("e c p -> e (c p)")
                             ).then_inc(comb_out, 16)
            sp.wait_ge(cT_ok, NS)
            sp.dma_start(rows[:, (NS - 1) * ST:], combT[:].rearrange("e c p -> e (c p)")).then_inc(comb_out, 16)
            sp.wait_ge(comb_out, 16 * NS)
            for j in range(EJ):
                sp.dma_start(comb_row[:, j, (NS - 1) * ST:], rows[j:j + 1, (NS - 1) * ST:].broadcast_to([P, ST])
                             ).then_inc(comb_load[j], 16)
            with sp.Fori(1, E // EJ) as i:
                for j in range(EJ):
                    sp.wait_ge(w1hi_ok, i * EJ + (j + 1 - EJ))
                    sp.wait_ge(w1lo_ok, i * EJ + (j + 1 - EJ))
                    sp.dma_start(w1_in[:, j, :], w1[bass.ds(i * EJ + j, 1), :, :].rearrange("e d f -> d (e f)")
                                 ).then_inc(w1_load[j], 16)
                    sp.wait_ge(w2hi_ok, i * EJ + (j + 1 - EJ))
                    sp.wait_ge(w2lo_ok, i * EJ + (j + 1 - EJ))
                    sp.dma_start(w2_in[:, j, :, :], w2[bass.ds(i * EJ + j, 1), :, :].rearrange("e (b p) d -> p (e b) d", p=P)
                                 ).then_inc(w2_load[j], 16)
                for j in range(EJ):
                    sp.wait_ge(part_ok, i * STEPS + (j + 1 - EJ) * NS)
                    sp.dma_start(comb_row[:, j, :], rows[bass.ds(i * EJ + j, 1), :].broadcast_to([P, T])
                                 ).then_inc(comb_load[j], 16)
            ov = out.rearrange("a (c p) d -> p (a c) d", p=P)
            for k in range(NS):
                sp.wait_ge(out_ok, k + 1)
                sp.dma_start(ov[:, k * SC:(k + 1) * SC, :], acc[:, k * SC:(k + 1) * SC, :]).then_inc(stored, 16)
            sp.wait_ge(stored, 16 * NS)

        @block.gpsimd
        def _(pool):
            pool.memset(neg_half[:], -0.5).then_inc(memsets, 1)
            pool.memset(state[:], 0.0).then_inc(memsets, 1)
            pool.memset(x_sb[:, NC:, :], 0.0).then_inc(memsets, 1)
            pool.memset(mv[:, NC:, :], 0.0).then_inc(memsets, 1)
            pool.memset(rstd[:, NC:], 0.0).then_inc(memsets, 1)
            pool.wait_ge(memsets, 5)
            for k in range(NS):
                pool.wait_ge(var1, k + 1)
                pool.tensor_tensor(rstd[:, k * SC:(k + 1) * SC], veps[:, k * SC:(k + 1) * SC],
                                   neg_half[:, 0:SC], ALU.pow).then_inc(rstd1_ok, 1)

            def normalise(i, c):
                pool.wait_ge(rden_ok, i * SC + c + 1)
                if c >= 2:
                    pool.wait_ge(oT_ps, i * 2 * SC + 2 * (c - 1))
                pool.tensor_tensor(on[:, c % 2, :, :], tcs[:, c % 2, :, 0:DH],
                                   rden[:, c % 2, :, None].broadcast_to([P, H, DH]), ALU.mult
                                   ).then_inc(on_ok, 1)

            def tail(i):
                pool.wait_ge(var2, i + 1)
                pool.tensor_tensor(rstd2[:], veps2[:], neg_half[:, 0:SC], ALU.pow).then_inc(rstd2_ok, 1)
                pool.wait_ge(yThi_ok, i + 1)
                pool.tensor_copy(yTall[:, 0, bass.ds(i * ST, ST)], f32(yT_hi[:])).then_inc(yT_all, 1)
                pool.wait_ge(yTlo_ok, i + 1)
                pool.tensor_copy(yTall[:, 1, bass.ds(i * ST, ST)], f32(yT_lo[:])).then_inc(yT_all, 1)

            for c in range(SC):
                normalise(0, c)
            with pool.Fori(1, NS) as i:
                tail(i - 1)
                for c in range(SC):
                    if c < 2:
                        pool.wait_ge(oT_ps, (i - 1) * 2 * SC + 2 * (c + SC - 1))
                    normalise(i, c)
            pool.wait_ge(o_ps, NS * GROUPS)
            pool.memset(accT[:], 0.0).then_inc(accT_zero, 1)
            pool.wait_ge(comb_out, 16 * (NS - 1))
            pool.wait_ge(v_rot, NS * V_JOBS)
            for j in range(EJ):
                pool.dma_start(comb_row[:, j, 0:(NS - 1) * ST], rows[j:j + 1, 0:(NS - 1) * ST]
                               .broadcast_to([P, (NS - 1) * ST])).then_inc(comb_early, 16)
            tail(NS - 1)

            def add(i, n):
                s = step(n)[1]
                pool.wait_ge(part_ok, i * STEPS + n + 1)
                pool.tensor_tensor(accT[:, s * ST:(s + 1) * ST], accT[:, s * ST:(s + 1) * ST],
                                   part[:, n % 2, :], ALU.add).then_inc(accT_ok, 1)

            pool.wait_ge(accT_zero, 1)
            for n in range(AHEAD - 1):
                add(0, n)
            with pool.Fori(0, E // EJ - 1) as i:
                for m in range(STEPS):
                    add(i, m + AHEAD - 1)
            for n in range(AHEAD - 1, NS):
                add(E // EJ - 1, n)

        @block.scalar
        def _(act):
            act.dma_start(brows[0:NP, :], bq.rearrange("(r p) -> r p", p=P)).then_inc(brow_in, 16)
            act.dma_start(brows[NP:2 * NP, :], bk.rearrange("(r p) -> r p", p=P)).then_inc(brow_in, 16)
            act.dma_start(brows[2 * NP:, :], b1.rearrange("e (b p) -> (e b) p", p=P)).then_inc(brow_in, 16)
            act.wait_ge(memsets, 1)
            act.activation(warm[:], neg_half[:, 0:1], ACT.Gelu)
            for k in (1, 2, 0):
                act.wait_ge(wl_in[k], 16)
                act.activation(w_hi[k][:], w_in[k], ACT.Copy).then_inc(whi_ok, 1)
                if k == 1:
                    act.wait_ge(bT_ps, 1)
                    act.activation(bcols[:], ps[:, 7, 0:2 * NP + E * FB], ACT.Copy).then_inc(bT_ok, 1)
                    act.wait_ge(xT_ps, 1)
                    act.activation(xT_hi[:], ps[:, 6, :], ACT.Copy).then_inc(xThi_ok, 1)
            act.wait_ge(row_in, 16 * 3)
            act.activation(gate_hi[:], gate_sb[:], ACT.Copy).then_inc(whi_ok, 1)
            act.wait_ge(bT_ok, 1)

            def turn_out(i, c):
                for half in range(2):
                    act.wait_ge(oT_ps, i * 2 * SC + 2 * c + half + 1)
                    act.activation(oT[:, c % 2, half * 4:half * 4 + 4, :],
                                   ps[:, 6 + half, :].rearrange("p (a b) -> p a b", b=P), ACT.Copy
                                   ).then_inc(oT_ok, 1)

            def front(i, tail):
                def keys(m):
                    act.wait_ge(kn_ps, i * K_JOBS + m + 1)
                    act.activation(kn[:, m // 2, (m % 2) * 512:(m % 2) * 512 + 512], ps[:, 5, :], ACT.Copy
                                   ).then_inc(kn_ok, 1)

                for j in range(QK_JOBS):
                    if j in K_AT:
                        keys(K_AT[j])
                    dst = (kT if j < NP else qT)[:, j % NP, :]
                    col = (NP if j < NP else 0) + j % NP
                    act.wait_ge(big_ps, i * QK_JOBS + j + 1)
                    act.activation(dst, ps[:, j % 4, :], ACT.Relu, bias=bcols[:, col:col + 1]).then_inc(big_ok, 1)
                    if tail and j == OT_AT:
                        turn_out(i - 1, SC - 1)
                    if tail and j == YT_AT:
                        act.wait_ge(yT_ps, i)
                        act.activation(yT_hi[:], ps[:, 6, :], ACT.Copy).then_inc(yThi_ok, 1)
                keys(K_JOBS - 1)

            def x_turned(i):
                act.wait_ge(xT_ps, i + 1)
                act.activation(xT_hi[:], ps[:, 6, :], ACT.Copy).then_inc(xThi_ok, 1)

            def comb_turned(i):
                act.wait_ge(cT_ps, i + 1)
                act.activation(combT[:], ps[0:E, 7, :].rearrange("p (a b) -> p a b", b=P), ACT.Copy).then_inc(cT_ok, 1)

            def cos_part(i, n):
                c = n // NG
                act.wait_ge(o_ps, i * GROUPS + n + 1)
                if n >= 2:
                    act.wait_ge(tcs_ok, i * GROUPS + n - 1)
                act.activation(tc[:, n % 2, :, :, :],
                               ps[:, 2 + 2 * (n % 2):4 + 2 * (n % 2), 0:2 * CS]
                               .rearrange("p a (b s v) -> p a b s v", b=2, s=2)[:, :, :, 0, :],
                               ACT.Copy, scale=cs4[:, 0, c:c + 1]).then_inc(tc_ok, 1)

            def attention(i, tail):
                for n in range(GROUPS - 1):
                    c, g = n // NG, n % NG
                    if g == 2 and c >= 1:
                        turn_out(i, c - 1)
                    cos_part(i, n)
                    if tail and n == 1:
                        act.wait_ge(gap_ok, i)
                        act.activation(th[:], gap[:], ACT.Tanh, scale=0.5).then_inc(th_ok, 1)
                    if tail and n == 3:
                        comb_turned(i - 1)
                    if n == GROUPS - 2:
                        x_turned(i + 1)
                if tail:
                    act.wait_ge(comb_out, i * 16)

            front(0, False)
            attention(0, False)
            with act.Fori(1, NS) as i:
                cos_part(i - 1, GROUPS - 1)
                front(i, True)
                attention(i, True)

            def w1_high(i, j):
                act.wait_ge(w1_load[j], i * 16 + 16)
                act.activation(b1_now[:, j * FB:(j + 1) * FB],
                               bcols[:, bass.ds((i * EJ + j) * FB + 2 * NP, FB)], ACT.Copy).then_inc(b1_ok, 1)
                act.activation(w1_hi[:, j, :], w1_in[:, j, :], ACT.Copy).then_inc(w1hi_ok, 1)

            def w2_high(i, j):
                act.wait_ge(w2_load[j], i * 16 + 16)
                act.activation(w2_hi[:, j, :, :], w2_in[:, j, :, :], ACT.Copy).then_inc(w2hi_ok, 1)

            def hidden(i, n, blocks=range(FB)):
                j = step(n)[0]
                if n % NS == 0:
                    act.wait_ge(b1_ok, i * EJ + n // NS + 1)
                for b in blocks:
                    act.wait_ge(h_ps, (i * STEPS + n) * FB + b + 1)
                    if n > 0:
                        act.wait_ge(hlo_ok, (i * STEPS + n - 1) * FB + b + 1)
                    act.activation(hT[:, b, :], ps[:, b, :], ACT.Gelu,
                                   bias=b1_now[:, j * FB + b:j * FB + b + 1]).then_inc(h_ok, 1)
                    if b >= 2:
                        odd = 1 if b == 2 else 3
                        if n >= 2 and b == 2:
                            act.wait_ge(y_ps, i * STEPS + n - 1)
                        act.wait_ge(h_ok, (i * STEPS + n) * FB + odd + 1)
                        act.activation(hT_hi[:, n % 2, odd, :], hT[:, odd, :], ACT.Copy).then_inc(hodd_ok, 1)

            w1_high(0, 0)
            cos_part(NS - 1, GROUPS - 1)
            act.wait_ge(o_ps, NS * GROUPS)
            w2_high(0, 0)
            hidden(0, 0)
            turn_out(NS - 1, SC - 1)
            w1_high(0, 1)
            hidden(0, 1)
            hidden(0, 2)
            act.wait_ge(yT_ps, NS)
            act.activation(yT_hi[:], ps[:, 6, :], ACT.Copy).then_inc(yThi_ok, 1)
            w2_high(0, 1)
            act.wait_ge(gap_ok, NS)
            act.activation(th[:], gap[:], ACT.Tanh, scale=0.5).then_inc(th_ok, 1)
            hidden(0, 3, blocks=range(0, 2))
            comb_turned(NS - 1)
            hidden(0, 3, blocks=range(2, FB))
            with act.Fori(0, E // EJ - 1) as i:
                for m in range(STEPS):
                    hidden(i, m + AHEAD)
                    if m % NS == 1:
                        w1_high(i + 1, m // NS)
                    if m % NS == 2:
                        act.wait_ge(y_ps, i * STEPS + (m // NS + 1) * NS)
                        w2_high(i + 1, m // NS)
            for n in range(AHEAD, STEPS):
                hidden(E // EJ - 1, n)

        @block.vector
        def _(dve):
            def norm1_stats(k):
                dve.wait_ge(x_in[k], 16)
                for c in range(k * SC, (k + 1) * SC):
                    last = dve.bn_stats(st6[:, c, :], x_sb[:, c, :])
                last.then_inc(bn1_ok, 1)
                dve.wait_ge(bn1_ok, k + 1)
                for c in range(k * SC, (k + 1) * SC):
                    last = dve.bn_aggr(mv[:, c, :], st6[:, c, :])
                last.then_inc(mv1_ok, 1)
                dve.wait_ge(mv1_ok, k + 1)
                dve.tensor_scalar(veps[:, k * SC:(k + 1) * SC], mv[:, k * SC:(k + 1) * SC, 1], EPS, None, ALU.add
                                  ).then_inc(var1, 1)

            def normed(i):
                for c in range(SC):
                    dve.tensor_scalar(xh[:, c, :], x_sb[:, bass.ds(i * SC + c, 1), :].rearrange("p a d -> p (a d)"),
                                      mv[:, bass.ds(i * SC + c, 1), 0], rstd[:, bass.ds(i * SC + c, 1)],
                                      ALU.subtract, ALU.mult).then_inc(xh_ok, 1)

            def low_half(k, count):
                dve.wait_ge(whi_ok, count)
                dve.tensor_tensor(w_lo[k][:], w_in[k], f32(w_hi[k][:]), ALU.subtract).then_inc(wlo_ok, 1)

            def angles(i):
                dve.tensor_copy(cs4[:], rot[:, :, bass.ds(i * SC, SC)]).then_inc(cs_ok, 1)

            def x_low(i):
                dve.wait_ge(xThi_ok, i + 1)
                dve.tensor_tensor(xT_lo[:], ps[:, 6, :], f32(xT_hi[:]), ALU.subtract).then_inc(xTlo_ok, 1)

            def ones_columns(i):
                dve.wait_ge(cs_ok, i + 1)
                for c in range(SC):
                    for s in range(2):
                        last = dve.tensor_copy(vcs[:, c, :, s, DH], cs4[:, s, c:c + 1].broadcast_to([P, H]))
                last.then_inc(vone, 1)

            def values(i, m):
                dve.wait_ge(v_ps, i * V_JOBS + m + 1)
                if m >= 2:
                    dve.wait_ge(v_rot, i * V_JOBS + m - 1)
                dve.tensor_tensor(vb[:, m % 2, :], ps[:, 4, :], bv_all[:, (m % 2) * 512:(m % 2) * 512 + 512],
                                  ALU.add).then_inc(v_add, 1)
                dve.wait_ge(v_add, i * V_JOBS + m + 1)
                for s in range(2):
                    last = dve.tensor_scalar(vcs[:, m // 2, (m % 2) * 8:(m % 2) * 8 + 8, s, 0:DH],
                                             vb[:, m % 2, :].rearrange("p (h d) -> p h d", d=DH),
                                             cs4[:, s, m // 2:m // 2 + 1], None, ALU.mult)
                last.then_inc(v_rot, 1)

            def front(i, tail):
                angles(i)
                ones_columns(i)
                for m in range(V_JOBS):
                    if m == V_JOBS - 1:
                        if not tail:
                            dve.wait_ge(c_in, 16 * 4)
                        masked(i, 0)
                    if not tail and 4 <= m < NS + 3:
                        norm1_stats(m - 3)
                    values(i, m)
                    if not tail and m == 0:
                        low_half(0, 3)
                        dve.wait_ge(whi_ok, 4)
                        dve.tensor_tensor(gate_lo[:], gate_sb[:], f32(gate_hi[:]), ALU.subtract).then_inc(wlo_ok, 1)
                    if tail and m == STATS_AFTER:
                        norm2_stats(i - 1)
                    if tail and m == NORM_AFTER:
                        norm2(i - 1)
                    if tail and m == NORMED_AFTER:
                        normed2(i - 1)
                    if tail and m == YLOW_AFTER:
                        y_low(i - 1)
                    if tail and m == BEST_AFTER:
                        best_two(i - 1)

            def masked(i, n):
                c = n // NG
                if n % NG == 0:
                    dve.wait_ge(pair_in[c], i * 16 + 16)
                dve.wait_ge(sc_ps, i * GROUPS + n + 1)
                if n >= 2:
                    dve.wait_ge(o_ps, i * GROUPS + n - 1)
                dve.tensor_tensor(am[:, n % 2, :, :].rearrange("p r (q t) -> p r q t", t=P),
                                  ps[:, 0:2, 0:2 * P].rearrange("p r (q t) -> p r q t", t=P),
                                  pair[:, c, None, None, :].broadcast_to([P, 2, 2, P]), ALU.mult).then_inc(am_ok, 1)

            def taken(i, n, opening=False):
                c, g = n // NG, n % NG
                ob = ps[:, 2 + 2 * (n % 2):4 + 2 * (n % 2), :]
                if g == 0 and c >= 2:
                    dve.wait_ge(on_ok, i * SC + c - 1)
                dve.wait_ge(tc_ok, i * GROUPS + n + 1)
                dve.tensor_tensor(state[:, 2 * g:2 * g + 2, :], ob[:, :, 2 * CS:3 * CS],
                                  state[:, 2 * g:2 * g + 2, :], ALU.add).then_inc(st_ok, 1)
                for r in range(2):
                    if opening:
                        last = dve.tensor_copy(tcs[:, c % 2, g * GH + r:(g + 1) * GH:2, :], tc[:, n % 2, r, :, :])
                        continue
                    last = dve.scalar_tensor_tensor(
                        out=tcs[:, c % 2, g * GH + r:(g + 1) * GH:2, :],
                        in0=ob[:, r, 0:2 * CS].rearrange("p (b s v) -> p b s v", b=2, s=2)[:, :, 1, :],
                        scalar=cs4[:, 1, c:c + 1], in1=tc[:, n % 2, r, :, :],
                        op0=ALU.mult, op1=ALU.add)
                last.then_inc(tcs_ok, 1)
                if g == NG - 1:
                    dve.wait_ge(tcs_ok, i * GROUPS + n + 1)
                    dve.tensor_scalar(dmax[:, c % 2, :], tcs[:, c % 2, :, DH], DEN_MIN, None, ALU.max
                                      ).then_inc(dmax_ok, 1)
                    dve.wait_ge(dmax_ok, i * SC + c + 1)
                    dve.reciprocal(rden[:, c % 2, :], dmax[:, c % 2, :]).then_inc(rden_ok, 1)

            def residual(i, c):
                dve.wait_ge(wo_ps, i * SC + c + 1)
                dve.tensor_tensor(x2[:, c, :], ps[:, 7, 0:D], x2[:, c, :], ALU.add).then_inc(x2_ok, 1)

            def norm2_stats(i):
                residual(i, SC - 1)
                dve.wait_ge(x2_ok, i * SC + SC)
                dve.memset(holder[:], 0.0)
                for c in range(SC):
                    last = dve.bn_stats(st62[:, c, :], x2[:, c, :])
                last.then_inc(bn2_ok, 1)

            def norm2(i):
                dve.wait_ge(bn2_ok, i + 1)
                dve.memset(holder[:], 0.0)
                for c in range(SC):
                    last = dve.bn_aggr(mv2[:, c, :], st62[:, c, :])
                last.then_inc(mv2_ok, 1)
                dve.wait_ge(mv2_ok, i + 1)
                dve.tensor_scalar(veps2[:], mv2[:, :, 1], EPS, None, ALU.add).then_inc(var2, 1)

            def normed2(i):
                dve.wait_ge(rstd2_ok, i + 1)
                for c in range(SC):
                    last = dve.tensor_scalar(yh[:, c, :], x2[:, c, :], mv2[:, c, 0:1], rstd2[:, c:c + 1],
                                             ALU.subtract, ALU.mult)
                last.then_inc(yh_ok, 1)

            def y_low(i):
                dve.wait_ge(yThi_ok, i + 1)
                dve.tensor_tensor(yT_lo[:], ps[:, 6, :], f32(yT_hi[:]), ALU.subtract).then_inc(yTlo_ok, 1)

            def best_two(i):
                dve.wait_ge(lg_ps, i + 1)
                dve.tensor_copy(lg[:], ps[:, 7, 0:SC * E].rearrange("p (c e) -> p c e", e=E)).then_inc(lg_ok, 1)
                dve.wait_ge(lg_ok, i + 1)
                dve.memset(holder[:], 0.0)
                for c in range(SC):
                    last = dve.max(top[:, c, :], lg[:, c, :])
                last.then_inc(top_ok, 1)
                dve.wait_ge(top_ok, i + 1)
                dve.tensor_tensor(gap[:], top[:, :, 0], top[:, :, 1], ALU.subtract).then_inc(gap_ok, 1)
                for c in range(SC):
                    last = dve.max_index(idx[:, c, :], top[:, c, :], lg[:, c, :])
                last.then_inc(idx_ok, 1)
                dve.wait_ge(idx_ok, i + 1)
                dve.tensor_copy(idxf[:], idx[:, :, 0:2]).then_inc(idxf_ok, 1)

            def combine(i):
                dve.wait_ge(idxf_ok, i + 1)
                dve.wait_ge(th_ok, i + 1)
                dve.tensor_scalar(wts[:, 0, :], th[:], 0.5, 0.5, ALU.mult, ALU.add)
                dve.tensor_scalar(wts[:, 1, :], th[:], -0.5, 0.5, ALU.mult, ALU.add).then_inc(wts_ok, 1)
                each = [P, 2, SC, E]
                dve.tensor_tensor(hot[:], iota[:, None, None, :].broadcast_to(each),
                                  idxf[:].rearrange("p c k -> p k c")[:, :, :, None].broadcast_to(each),
                                  ALU.is_equal).then_inc(hot_ok, 1)
                dve.wait_ge(wts_ok, i + 1)
                dve.wait_ge(hot_ok, i + 1)
                dve.tensor_tensor(hot[:], hot[:], wts[:, :, :, None].broadcast_to(each), ALU.mult).then_inc(hotw_ok, 1)
                dve.wait_ge(hotw_ok, i + 1)
                dve.tensor_tensor(comb[:], hot[:, 0, :, :], hot[:, 1, :, :], ALU.add).then_inc(comb_ok, 1)

            def open_sum(i):
                dve.wait_ge(b2_ps, i + 1)
                dve.tensor_tensor(acc[:, bass.ds(i * SC, SC), :], ps[:, 6, :].rearrange("p (c d) -> p c d", d=D),
                                  x2[:], ALU.add).then_inc(acc0_ok, 1)

            def open_residual(i):
                dve.tensor_tensor(x2[:], x_sb[:, bass.ds(i * SC, SC), :],
                                  bo_all[:, None, :].broadcast_to([P, SC, D]), ALU.add).then_inc(x2_open, 1)

            def finish(i):
                taken(i, GROUPS - 1)
                residual(i, SC - 2)

            def attention(i, tail):
                for n in range(GROUPS):
                    if tail and n == 6:
                        open_sum(i - 1)
                        dve.wait_ge(acc0_ok, i)
                    if n >= 1:
                        masked(i, n)
                        taken(i, n - 1, opening=not tail and n <= NG)
                    if tail and n == 3:
                        combine(i - 1)
                    if n == 7:
                        open_residual(i)
                    if n == 2 * NG:
                        if not tail:
                            dve.wait_ge(rstd1_ok, NS)
                        normed(i + 1)
                    if n % NG == 1 and n > 2 * NG:
                        if n // NG == 2:
                            dve.wait_ge(x2_open, i + 1)
                        residual(i, n // NG - 2)
                x_low(i + 1)

            norm1_stats(0)
            dve.wait_ge(rstd1_ok, 1)
            normed(0)
            low_half(1, 1)
            x_low(0)
            low_half(2, 2)
            dve.wait_ge(row_in, 16 * 3)
            front(0, False)
            dve.wait_ge(memsets, 5)
            attention(0, False)
            with dve.Fori(1, NS) as i:
                finish(i - 1)
                front(i, True)
                attention(i, True)

            def w1_low(i, j):
                dve.wait_ge(w1hi_ok, i * EJ + j + 1)
                dve.tensor_tensor(w1_lo[:, j, :], w1_in[:, j, :], f32(w1_hi[:, j, :]), ALU.subtract
                                  ).then_inc(w1lo_ok, 1)

            def w2_low(i, j):
                dve.wait_ge(w2hi_ok, i * EJ + j + 1)
                dve.tensor_tensor(w2_lo[:, j, :, :], w2_in[:, j, :, :], f32(w2_hi[:, j, :, :]), ALU.subtract
                                  ).then_inc(w2lo_ok, 1)

            def halves(i, n):
                if n >= 2:
                    dve.wait_ge(y_ps, i * STEPS + n - 1)

                def low(b):
                    dve.wait_ge(hodd_ok if b % 2 else heven_ok, (i * STEPS + n) * (FB // 2) + b // 2 + 1)
                    dve.tensor_tensor(hT_lo[:, n % 2, b, :], hT[:, b, :], f32(hT_hi[:, n % 2, b, :]), ALU.subtract
                                      ).then_inc(hlo_ok, 1)
                for b in range(0, FB, 2):
                    dve.wait_ge(h_ok, (i * STEPS + n) * FB + b + 1)
                    dve.tensor_copy(hT_hi[:, n % 2, b, :], hT[:, b, :]).then_inc(heven_ok, 1)
                    if b:
                        low(b - 1)
                    low(b)
                low(FB - 1)

            def weigh(i, n, early=False, last=False):
                j, s = step(n)
                dve.wait_ge(y_ps, i * STEPS + n + 1)
                if n >= 2 and not last:
                    dve.wait_ge(accT_ok, i * STEPS + n - 1)
                if last and s >= 2:
                    dve.wait_ge(accT_end, s - 1)
                if not early and s in (0, NS - 1):
                    dve.wait_ge(comb_load[j], (i + n // STEPS) * 16 + 16)
                dve.tensor_tensor(part[:, n % 2, :], ps[:, 4 + n % 2, :], comb_row[:, j, s * ST:(s + 1) * ST],
                                  ALU.mult).then_inc(part_ok, 1)

            def add_last(k):
                dve.wait_ge(accT_ok, E * NS - NS)
                dve.wait_ge(part_ok, E * NS - NS + k + 1)
                dve.tensor_tensor(accT[:, k * ST:(k + 1) * ST], accT[:, k * ST:(k + 1) * ST],
                                  part[:, k % 2, :], ALU.add).then_inc(accT_end, 1)

            def store(k):
                dve.wait_ge(back_ps, k + 1)
                dve.tensor_tensor(acc[:, k * SC:(k + 1) * SC, :], ps[:, 6 + k % 2, :].rearrange("p (c d) -> p c d", d=D),
                                  acc[:, k * SC:(k + 1) * SC, :], ALU.add).then_inc(out_ok, 1)

            w1_low(0, 0)
            finish(NS - 1)
            dve.wait_ge(o_ps, NS * GROUPS)
            w2_low(0, 0)
            halves(0, 0)
            w1_low(0, 1)
            halves(0, 1)
            norm2_stats(NS - 1)
            norm2(NS - 1)
            normed2(NS - 1)
            dve.wait_ge(comb_early, 16 * EJ)
            weigh(0, 0, early=True)
            halves(0, 2)
            y_low(NS - 1)
            w2_low(0, 1)
            weigh(0, 1, early=True)
            best_two(NS - 1)
            combine(NS - 1)
            weigh(0, 2, early=True)
            halves(0, 3)
            open_sum(NS - 1)
            with dve.Fori(0, E // EJ - 1) as i:
                for m in range(STEPS):
                    halves(i, m + AHEAD)
                    weigh(i, m + AHEAD - 1)
                    if m % NS == 1:
                        w1_low(i + 1, m // NS)
                    if m % NS == 2:
                        w2_low(i + 1, m // NS)
            for n in range(AHEAD - 1, STEPS):
                if n + 1 < STEPS:
                    halves(E // EJ - 1, n + 1)
                if n > NS:
                    add_last(n - NS - 1)
                weigh(E // EJ - 1, n, last=n >= NS + 2)
                if n > NS + 1:
                    store(n - NS - 2)
            add_last(NS - 1)
            store(NS - 2)
            store(NS - 1)

        @block.tensor
        def _(pe):
            mm = pe.matmul
            def split3(o, a, b, part_a, part_b):
                mm(o, part_a(a[0]), part_b(b[0]), start=True, stop=False)
                mm(o, part_a(a[0]), part_b(b[1]), start=False, stop=False)
                return mm(o, part_a(a[1]), part_b(b[0]), start=False, stop=True)

            def turn_x(i):
                for c in range(SC):
                    pe.wait_ge(xh_ok, i * SC + c + 1)
                    last = pe.transpose(ps[:, 6, c * P:(c + 1) * P], xh[:, c, :], ident[:])
                last.then_inc(xT_ps, 1)

            def front(i, tail):
                pe.wait_ge(xThi_ok, i + 1)
                pe.wait_ge(xTlo_ok, i + 1)

                def block(j):
                    if j >= 4:
                        pe.wait_ge(big_ok, i * QK_JOBS + j - 3)
                    if not tail and j == NP:
                        pe.wait_ge(whi_ok, 3)
                        pe.wait_ge(wlo_ok, 3)
                    w, b = 1 if j < NP else 0, j % NP
                    split3(ps[:, j % 4, :], (w_hi[w], w_lo[w]), (xT_hi, xT_lo),
                           lambda t: t[:, b * P:(b + 1) * P], lambda t: t[:]).then_inc(big_ps, 1)

                def values(m):
                    if m >= 1:
                        pe.wait_ge(v_add, i * V_JOBS + m)
                    if not tail and m == 0:
                        pe.wait_ge(whi_ok, 2)
                        pe.wait_ge(wlo_ok, 2)
                    c, half = m // 2, m % 2
                    split3(ps[:, 4, :], (xT_hi, xT_lo), (w_hi[2], w_lo[2]),
                           lambda t: t[:, c * P:(c + 1) * P], lambda t: t[:, half * 512:half * 512 + 512]
                           ).then_inc(v_ps, 1)

                def keys(m):
                    if m == 0:
                        pe.wait_ge(big_ok, i * QK_JOBS + NP)
                    else:
                        pe.wait_ge(kn_ok, i * K_JOBS + m)
                    for q in range(4):
                        last = pe.transpose(ps[:, 5, q * P:(q + 1) * P],
                                            kT[:, (m % 2) * 4 + q, m // 2 * P:(m // 2 + 1) * P], ident[:])
                    last.then_inc(kn_ps, 1)

                for j in range(QK_JOBS):
                    if tail and j == 2:
                        pe.wait_ge(tcs_ok, i * GROUPS)
                    if j in K_AT:
                        keys(K_AT[j])
                    block(j)
                    if j in V_AT:
                        values(V_AT[j])
                    if tail and j == OT_AT:
                        turn_out(i - 1, SC - 1)
                    if tail and j == WO_AT:
                        project(i - 1, SC - 1)
                    if tail and j == YT_AT:
                        turn_y(i - 1)
                    if tail and j == GATE_AT:
                        gate(i - 1)
                scores(i, 0)
                values(V_JOBS - 1)
                keys(K_JOBS - 1)

            def scores(i, n):
                if n == 0:
                    pe.wait_ge(big_ok, i * QK_JOBS + QK_JOBS - 2)
                c, g = n // NG, n % NG
                if n >= 1:
                    pe.wait_ge(am_ok, i * GROUPS + n)
                for h in range(g * GH, (g + 1) * GH):
                    r = slice(64 * (h % 2), 64 * (h % 2) + 64)
                    col = (h % GH) // 2 * P
                    last = mm(ps[:, h % 2, col:col + P], kT[r, h // 2, c * P:(c + 1) * P],
                              qT[r, h // 2, c * P:(c + 1) * P], start=True, stop=True)
                last.then_inc(sc_ps, 1)

            def outputs(i, n, opening=False):
                c, g = n // NG, n % NG
                pe.wait_ge(am_ok, i * GROUPS + n + 1)
                if n == 0:
                    pe.wait_ge(big_ok, i * QK_JOBS + QK_JOBS)
                if n == 1:
                    pe.wait_ge(v_add, i * V_JOBS + V_JOBS)
                    pe.wait_ge(kn_ok, i * K_JOBS + K_JOBS)
                if n >= 2:
                    pe.wait_ge(tcs_ok, i * GROUPS + n - 1)
                    pe.wait_ge(st_ok, i * GROUPS + n - 1)
                if c >= 1:
                    pe.wait_ge(st_ok, i * GROUPS + n - NG + 1)
                if g == 0:
                    pe.wait_ge(v_rot, i * V_JOBS + 2 * c + 2)
                    pe.wait_ge(kn_ok, i * K_JOBS + 2 * c + 2)
                    pe.wait_ge(vone, i + 1)
                vh = lambda h: vcs[:, c, h, :, :].rearrange("p s v -> p (s v)")
                for h in range(g * GH, (g + 1) * GH):
                    q, r = h % GH // 2, h % 2
                    for t in (64, 0):
                        mm(ps[t:t + 64, 2 + 2 * (n % 2) + r, q * CS:q * CS + VW],
                           am[:, n % 2, r, q * P + t:q * P + t + 64], vcs[:, c, h, 0, :],
                           start=(q == 0), stop=opening, skip_group_check=True)
                for h in range(g * GH, g * GH if opening else (g + 1) * GH):
                    q, r = h % GH // 2, h % 2
                    rows = slice(64 * r, 64 * r + 64)
                    mm(ps[:, 2 + 2 * (n % 2) + r, q * CS:(q + 1) * CS], qT[rows, h // 2, c * P:(c + 1) * P],
                       state[rows, h // 2, :], start=False, stop=True, skip_group_check=True)
                for h in (1, 0, 3, 2):
                    h += g * GH
                    q, r = h % GH // 2, h % 2
                    last = mm(ps[64 * r:64 * r + 64, 2 + 2 * (n % 2) + q, 2 * CS:3 * CS],
                              kn[:, c, h * DH:(h + 1) * DH], vh(h), start=True, stop=True, skip_group_check=True)
                last.then_inc(o_ps, 1)

            def turn_out(i, c):
                pe.wait_ge(on_ok, i * SC + c + 1)
                for half in range(2):
                    if half == 1 and c >= 1:
                        pe.wait_ge(x2_ok, i * SC + c)
                    for q in range(4):
                        pr = half * 4 + q
                        last = pe.transpose(ps[:, 6 + half, q * P:(q + 1) * P],
                                            on[:, c % 2, 2 * pr:2 * pr + 2, :].rearrange("p h d -> p (h d)"),
                                            ident[:])
                    last.then_inc(oT_ps, 1)

            def project(i, c):
                pe.wait_ge(oT_ok, i * 2 * SC + 2 * c + 2)
                for pr in range(NP):
                    last = mm(ps[:, 7, 0:D], oT[:, c % 2, pr, :], wo_sb[:, pr, :], start=(pr == 0), stop=(pr == NP - 1))
                last.then_inc(wo_ps, 1)

            def turn_y(i):
                pe.wait_ge(yh_ok, i + 1)
                for c in range(SC):
                    last = pe.transpose(ps[:, 6, c * P:(c + 1) * P], yh[:, c, :], ident[:])
                last.then_inc(yT_ps, 1)

            def gate(i):
                pe.wait_ge(yThi_ok, i + 1)
                pe.wait_ge(yTlo_ok, i + 1)
                for c in range(SC):
                    last = split3(ps[:, 7, c * E:(c + 1) * E], (yT_hi, yT_lo), (gate_hi, gate_lo),
                                  lambda t: t[:, c * P:(c + 1) * P], lambda t: t[:])
                last.then_inc(lg_ps, 1)

            def turn_comb(i):
                pe.wait_ge(comb_ok, i + 1)
                for c in range(SC):
                    last = pe.transpose(ps[0:E, 7, c * P:(c + 1) * P], comb[:, c, :], ident[:])
                last.then_inc(cT_ps, 1)

            def biases(i):
                pe.wait_ge(cT_ok, i + 1)
                for c in range(SC):
                    last = mm(ps[:, 6, c * D:(c + 1) * D], combT[:, c, :], b2_sb[:], start=True, stop=True)
                last.then_inc(b2_ps, 1)

            def attention(i, tail):
                for n in range(GROUPS + 1):
                    if 1 <= n < GROUPS:
                        scores(i, n)
                    if n >= 1:
                        outputs(i, n - 1, opening=not tail and n <= NG)
                    if tail and n == 4:
                        turn_comb(i - 1)
                    if tail and n == 5:
                        biases(i - 1)
                    if n % NG == 2 and n >= NG:
                        if n // NG == 1 and tail:
                            pe.wait_ge(acc0_ok, i)
                        turn_out(i, n // NG - 1)
                    if n % NG == 0 and n >= 2 * NG:
                        project(i, n // NG - 2)
                    if n == GROUPS - 1:
                        pe.wait_ge(oT_ok, i * 2 * SC + 2 * (SC - 1))
                        turn_x(i + 1)

            pe.wait_ge(brow_in, 16 * 4)
            pe.transpose(ps[:, 7, 0:2 * NP + E * FB], brows[:], ident[0:2 * NP + E * FB, 0:2 * NP + E * FB]
                         ).then_inc(bT_ps, 1)
            turn_x(0)
            pe.wait_ge(bT_ok, 1)
            pe.wait_ge(whi_ok, 1)
            pe.wait_ge(wlo_ok, 1)
            front(0, False)
            attention(0, False)
            with pe.Fori(1, NS) as i:
                front(i, True)
                attention(i, True)

            def hidden(i, n, first=False, blocks=range(FB)):
                j, s = step(n)
                if s == 0:
                    pe.wait_ge(w1hi_ok, i * EJ + n // NS + 1)
                    pe.wait_ge(w1lo_ok, i * EJ + n // NS + 1)
                for b in blocks:
                    if first and b == 2:
                        pe.wait_ge(tcs_ok, NS * GROUPS)
                        pe.wait_ge(st_ok, NS * GROUPS)
                    if n > 0:
                        pe.wait_ge(h_ok, (i * STEPS + n - 1) * FB + b + 1)
                    split3(ps[:, b, :], (w1_hi, w1_lo), (0, 1),
                           lambda t: t[:, j, b * P:(b + 1) * P], lambda t: yTall[:, t, s * ST:(s + 1) * ST]
                           ).then_inc(h_ps, 1)

            def down(i, n, blocks=range(FB)):
                j, s = step(n)
                if s == 0:
                    pe.wait_ge(w2hi_ok, i * EJ + n // NS + 1)
                    pe.wait_ge(w2lo_ok, i * EJ + n // NS + 1)
                if n >= 2:
                    pe.wait_ge(part_ok, i * STEPS + n - 1)
                o = ps[:, 4 + n % 2, :]
                for b in blocks:
                    pe.wait_ge(hlo_ok, (i * STEPS + n) * FB + b + 1)
                    mm(o, w2_hi[:, j, b, :], hT_hi[:, n % 2, b, :], start=(b == 0), stop=False)
                    mm(o, w2_hi[:, j, b, :], hT_lo[:, n % 2, b, :], start=False, stop=False)
                    last = mm(o, w2_lo[:, j, b, :], hT_hi[:, n % 2, b, :], start=False, stop=(b == FB - 1))
                if blocks[-1] == FB - 1:
                    last.then_inc(y_ps, 1)

            def turn_back(k):
                if k >= 2:
                    pe.wait_ge(out_ok, k - 1)
                pe.wait_ge(accT_end, k + 1)
                for c in range(SC):
                    last = pe.transpose(ps[:, 6 + k % 2, c * D:(c + 1) * D],
                                        accT[:, k * ST + c * P:k * ST + (c + 1) * P], ident[:])
                last.then_inc(back_ps, 1)

            pe.wait_ge(am_ok, NS * GROUPS)
            pe.wait_ge(yT_all, 2 * (NS - 1))
            hidden(0, 0, first=True)
            pe.wait_ge(xThi_ok, NS + 1)
            pe.wait_ge(xTlo_ok, NS + 1)
            turn_out(NS - 1, SC - 1)
            hidden(0, 1)
            project(NS - 1, SC - 1)
            down(0, 0)
            hidden(0, 2)
            down(0, 1)
            turn_y(NS - 1)
            down(0, 2, blocks=range(0, 3))
            gate(NS - 1)
            down(0, 2, blocks=range(3, FB))
            pe.wait_ge(yT_all, 2 * NS)
            hidden(0, 3, blocks=range(0, 2))
            turn_comb(NS - 1)
            hidden(0, 3, blocks=range(2, FB))
            biases(NS - 1)
            with pe.Fori(0, E // EJ - 1) as i:
                for m in range(STEPS):
                    hidden(i, m + AHEAD)
                    down(i, m + AHEAD - 1)
            pe.wait_ge(acc0_ok, NS)
            for n in range(AHEAD - 1, STEPS):
                if n + 1 < STEPS:
                    hidden(E // EJ - 1, n + 1)
                down(E // EJ - 1, n)
                if n > NS + 1:
                    turn_back(n - NS - 2)
            turn_back(NS - 2)
            turn_back(NS - 1)


_INS = ["L0_attn_x", "L0_attn_Wq", "L0_attn_bq", "L0_attn_Wk", "L0_attn_bk", "L0_attn_Wv", "L0_attn_bv",
        "L0_attn_Wo", "L0_attn_bo", "L0_ffn_gate_w", "L0_ffn_w1", "L0_ffn_b1", "L0_ffn_w2", "L0_ffn_b2"]


def shape_constants():
    angles = np.float32(math.pi / (2.0 * T)) * np.arange(T, dtype=np.float32)
    rot = np.stack([np.cos(angles), np.sin(angles)]).astype(np.float32)
    rot = np.ascontiguousarray(rot.reshape(2, NC, P).transpose(2, 0, 1).reshape(P, 2 * NC))
    cos, sin = np.cos(angles).reshape(NC, P), np.sin(angles).reshape(NC, P)
    tan = (sin.astype(np.float64) / cos.astype(np.float64))
    pair = (1.0 + tan[:, :, None] * tan[:, None, :]) * np.triu(np.ones((P, P)))
    pair = np.ascontiguousarray(pair.transpose(1, 0, 2).astype(np.float32))
    iota = np.tile(np.arange(E, dtype=np.float32), (P, 1))
    return {"c_rot": rot, "c_pair": pair, "c_ident": np.eye(P, dtype=np.float32), "c_iota": iota}


def kernel(**inputs):
    import concourse.bacc as bacc
    from concourse.bass_utils import run_bass_kernel_spmd

    nc = bacc.Bacc("TRN2", target_bir_lowering=False, num_devices=1)
    arrays = {f"in_{name}": np.ascontiguousarray(inputs[name]) for name in _INS}
    arrays.update(shape_constants())
    args = [nc.dram_tensor(n, a.shape, mybir.dt.from_np(a.dtype), kind="ExternalInput").ap()
            for n, a in arrays.items()]
    out = nc.dram_tensor("out", (1, T, D), F32, kind="ExternalOutput").ap()
    rows = nc.dram_tensor("rows", (E, T), F32).ap()
    moe_block(nc, *args, out, rows)
    r = run_bass_kernel_spmd(nc, [arrays], core_ids=[0])
    return r.results[0]["out"]
```
